# Optimizing a Trainium2 kernel written in Bass

```python
import numpy as np
import jax
import jax.numpy as jnp

def _softmax(x, axis=-1):
    return jax.nn.softmax(x, axis=axis)

def _gelu(x):
    return jax.nn.gelu(x, approximate=True)

def _silu(x):
    return jax.nn.silu(x)

def _sigmoid(x):
    return jax.nn.sigmoid(x)

def _layernorm(x, axis=-1, eps=1e-05):
    m = jnp.mean(x, axis=axis, keepdims=True)
    v = jnp.var(x, axis=axis, keepdims=True)
    return (x - m) / jnp.sqrt(v + eps)

def _scatter_add(tgt, idx, src, axis=0):
    return tgt.at[idx].add(src)

def _segment_sum(src, seg, n):
    return jax.ops.segment_sum(src, seg, n)
kernel_name = 'mk_conv_attn_hybrid_d2_conv_nhwc128_r4_6db261'

def setup_inputs(seed: int=0):
    np.random.seed(seed)
    _w = jnp.asarray

    def _rec_inputs():
        import jax
        import jax.numpy as jnp
        _gk = jax.random.key(seed)
        x = -0.0003957 + 1 * jax.random.normal(jax.random.fold_in(_gk, 1), (32, 56, 56, 32), jnp.float32)
        return x
    x = _rec_inputs()

    def _L0_conv_setup():
        import jax, jax.numpy as jnp
        import numpy as np
        from jax import lax
        EPS = 0.001

        def _sign_pm1(v):
            return jnp.where(v >= 0, jnp.ones_like(v), -jnp.ones_like(v))
        key = jax.random.key(seed)
        k1, k2 = jax.random.split(key)
        B, H, Wd, Cin, Cout, KS = (32, 56, 56, 32, 32, 3)
        x = jax.random.normal(k1, (B, H, Wd, Cin), dtype=jnp.float32)
        gamma = jnp.ones((Cin,), dtype=jnp.float32)
        beta = jnp.zeros((Cin,), dtype=jnp.float32)
        W = jax.random.normal(k2, (KS, KS, Cin, Cout), dtype=jnp.float32) * 0.1
        return {'x': x, 'gamma': gamma, 'beta': beta, 'W': W}
    _L0_conv_all = _L0_conv_setup()
    _L0_conv_in = {k: v for k, v in _L0_conv_all.items() if k in ('gamma', 'beta', 'W')}
    del _L0_conv_all

    def _L1_attn_setup():
        import jax, jax.numpy as jnp
        import numpy as np
        B, S, D, H = (4, 1024, 32, 16)
        DH = D * H
        key = jax.random.key(seed)
        ks = jax.random.split(key, 10)
        sc = lambda fan: 1.0 / np.sqrt(fan)
        return {'x': jax.random.normal(ks[0], (B, S, D), jnp.float32), 'mask': jnp.ones((B, S), jnp.bool_), 'wq_w': jax.random.normal(ks[1], (DH, D), jnp.float32) * sc(D), 'wq_b': jax.random.normal(ks[2], (DH,), jnp.float32) * 0.01, 'wk_w': jax.random.normal(ks[3], (DH, D), jnp.float32) * sc(D), 'wk_b': jax.random.normal(ks[4], (DH,), jnp.float32) * 0.01, 'wv_w': jax.random.normal(ks[5], (DH, D), jnp.float32) * sc(D), 'wv_b': jax.random.normal(ks[6], (DH,), jnp.float32) * 0.01, 'dense_w': jax.random.normal(ks[7], (D, DH), jnp.float32) * sc(DH), 'dense_b': jax.random.normal(ks[8], (D,), jnp.float32) * 0.01}
    _L1_attn_all = _L1_attn_setup()
    _L1_attn_in = {k: v for k, v in _L1_attn_all.items() if k in ('mask', 'wq_w', 'wq_b', 'wk_w', 'wk_b', 'wv_w', 'wv_b', 'dense_w', 'dense_b')}
    del _L1_attn_all

    def _L1_ffn_setup():
        import jax, jax.numpy as jnp
        import numpy as np
        B, N, D, C, E, K = (8, 2048, 32, 32, 8, 2)
        key = jax.random.key(seed)
        k0, k1, k2 = jax.random.split(key, 3)
        x = jax.random.normal(k0, (B, N, D), dtype=jnp.float32)
        router_w = jax.random.normal(k1, (D, E), dtype=jnp.float32) * 0.05
        router_b = jnp.zeros((E,), dtype=jnp.float32)
        expert_w = jax.random.normal(k2, (E, D, C), dtype=jnp.float32) * (1.0 / np.sqrt(D))
        expert_b = jnp.zeros((E, C), dtype=jnp.float32)
        return {'x': x, 'router_w': router_w, 'router_b': router_b, 'expert_w': expert_w, 'expert_b': expert_b}
    _L1_ffn_all = _L1_ffn_setup()
    _L1_ffn_in = {k: v for k, v in _L1_ffn_all.items() if k in ('router_w', 'router_b', 'expert_w', 'expert_b')}
    del _L1_ffn_all
    return {'x': x, 'L0_conv_gamma': _L0_conv_in['gamma'], 'L0_conv_beta': _L0_conv_in['beta'], 'L0_conv_W': _L0_conv_in['W'], 'L1_attn_mask': _L1_attn_in['mask'], 'L1_attn_wq_w': _L1_attn_in['wq_w'], 'L1_attn_wq_b': _L1_attn_in['wq_b'], 'L1_attn_wk_w': _L1_attn_in['wk_w'], 'L1_attn_wk_b': _L1_attn_in['wk_b'], 'L1_attn_wv_w': _L1_attn_in['wv_w'], 'L1_attn_wv_b': _L1_attn_in['wv_b'], 'L1_attn_dense_w': _L1_attn_in['dense_w'], 'L1_attn_dense_b': _L1_attn_in['dense_b'], 'L1_ffn_router_w': _L1_ffn_in['router_w'], 'L1_ffn_router_b': _L1_ffn_in['router_b'], 'L1_ffn_expert_w': _L1_ffn_in['expert_w'], 'L1_ffn_expert_b': _L1_ffn_in['expert_b']}

def reference(x, L0_conv_gamma, L0_conv_beta, L0_conv_W, L1_attn_mask, L1_attn_wq_w, L1_attn_wq_b, L1_attn_wk_w, L1_attn_wk_b, L1_attn_wv_w, L1_attn_wv_b, L1_attn_dense_w, L1_attn_dense_b, L1_ffn_router_w, L1_ffn_router_b, L1_ffn_expert_w, L1_ffn_expert_b):
    import jax
    import jax.numpy as jnp

    def _L0_conv_ref(x, gamma, beta, W):
        import jax, jax.numpy as jnp
        import numpy as np
        from jax import lax
        EPS = 0.001

        def _sign_pm1(v):
            return jnp.where(v >= 0, jnp.ones_like(v), -jnp.ones_like(v))
        axes = (0, 1, 2)
        mean = jnp.mean(x, axis=axes, keepdims=True)
        var = jnp.var(x, axis=axes, keepdims=True)
        x_hat = (x - mean) * lax.rsqrt(var + EPS)
        out_bn = gamma * x_hat + beta
        x_bin = _sign_pm1(out_bn)
        scale = jnp.mean(jnp.abs(W), axis=(0, 1, 2))
        W_bin = _sign_pm1(W) * scale
        x_pad = jnp.pad(x_bin, ((0, 0), (1, 1), (1, 1), (0, 0)), constant_values=1.0)
        out = lax.conv_general_dilated(x_pad, W_bin, window_strides=(1, 1), padding='VALID', dimension_numbers=('NHWC', 'HWIO', 'NHWC'))
        return out

    def _L1_attn_ref(x, mask, wq_w, wq_b, wk_w, wk_b, wv_w, wv_b, dense_w, dense_b):
        import jax, jax.numpy as jnp
        import numpy as np
        B, S, D, H = (4, 1024, 32, 16)
        DH = D * H
        b, s, d = x.shape
        h = wq_w.shape[0] // d
        q = (x @ wq_w.T + wq_b).reshape(b, s, h, d)
        k = (x @ wk_w.T + wk_b).reshape(b, s, h, d)
        v = (x @ wv_w.T + wv_b).reshape(b, s, h, d)
        q = jax.nn.elu(q) + 1.0
        k = jax.nn.elu(k) + 1.0
        pos = 1.57 * jnp.arange(s, dtype=x.dtype) / s
        cos = jnp.cos(pos)[None, :, None, None]
        sin = jnp.sin(pos)[None, :, None, None]
        q_cos, q_sin = (q * cos, q * sin)
        k_cos, k_sin = (k * cos, k * sin)
        kv_cos = jnp.einsum('bshx,bshz->bhxz', k_cos, v)
        kv_sin = jnp.einsum('bshx,bshz->bhxz', k_sin, v)
        qkv = jnp.einsum('bshx,bhxz->bshz', q_cos, kv_cos) + jnp.einsum('bshx,bhxz->bshz', q_sin, kv_sin)
        denom = 1.0 / (jnp.einsum('bshd,bhd->bsh', q_cos, k_cos.sum(axis=1)) + jnp.einsum('bshd,bhd->bsh', q_sin, k_sin.sum(axis=1)) + 1e-05)
        o = qkv * denom[..., None]
        concat = o.reshape(b, s, h * d)
        return concat @ dense_w.T + dense_b

    def _L1_ffn_ref(x, router_w, router_b, expert_w, expert_b):
        import jax, jax.numpy as jnp
        import numpy as np
        B, N, D, C, E, K = (8, 2048, 32, 32, 8, 2)
        router_probs = jax.nn.softmax(x @ router_w + router_b, axis=-1)
        top_p, top_i = jax.lax.top_k(router_probs, K)
        top_p = top_p / jnp.sum(top_p, axis=-1, keepdims=True)
        expert_out = jnp.einsum('bnd,edc->bnec', x, expert_w) + expert_b
        gathered = jnp.take_along_axis(expert_out, top_i[..., None], axis=2)
        return jnp.einsum('bnk,bnkc->bnc', top_p, gathered)

    def _gn(v, G=32, eps=1e-05):
        B_, H_, W_, C_ = v.shape
        g = v.reshape(B_, H_, W_, G, C_ // G)
        m = jnp.mean(g, axis=(1, 2, 4), keepdims=True)
        s = jnp.var(g, axis=(1, 2, 4), keepdims=True)
        return ((g - m) / jnp.sqrt(s + eps)).reshape(v.shape)

    def _ln_c(v, eps=1e-06):
        m = jnp.mean(v, axis=-1, keepdims=True)
        s = jnp.var(v, axis=-1, keepdims=True)
        return (v - m) / jnp.sqrt(s + eps)

    def _ln_t(v, eps=1e-05):
        m = jnp.mean(v, axis=-1, keepdims=True)
        s = jnp.var(v, axis=-1, keepdims=True)
        return (v - m) / jnp.sqrt(s + eps)

    def _to_tokens(v):
        B_, H_, W_, C_ = v.shape
        return v.reshape(B_, H_ * W_, C_)

    def _from_tokens(t, like):
        return t.reshape(like.shape)
    x = x + _L0_conv_ref(_gn(x), L0_conv_gamma, L0_conv_beta, L0_conv_W)
    t = _to_tokens(x)
    t = t + _L1_attn_ref(_ln_t(t), L1_attn_mask, L1_attn_wq_w, L1_attn_wq_b, L1_attn_wk_w, L1_attn_wk_b, L1_attn_wv_w, L1_attn_wv_b, L1_attn_dense_w, L1_attn_dense_b)
    t = t + _L1_ffn_ref(_ln_t(t), L1_ffn_router_w, L1_ffn_router_b, L1_ffn_expert_w, L1_ffn_expert_b)
    x = _from_tokens(t, x)
    return x

_drawn_inputs = setup_inputs


def setup_inputs(seed=0):
    import zlib

    import numpy as np

    out = dict(_drawn_inputs(seed))
    spreads = {'L0_conv_gamma': (1.0, 0.2),
     'L0_conv_beta': (0.0, 0.1),
     'L1_ffn_router_b': (0.0, 0.1),
     'L1_ffn_expert_b': (0.0, 0.1)}
    factors = {'L1_attn_wq_b': 51.562, 'L1_attn_wk_b': 64.0}
    for name, (base, spread) in spreads.items():
        noise = np.random.default_rng([zlib.crc32(name.encode()), seed]).standard_normal(out[name].shape)
        drawn = base * np.exp(spread * noise) if base else spread * noise
        out[name] = jnp.asarray(drawn.astype(out[name].dtype))
    for name, factor in factors.items():
        out[name] = (out[name] * factor).astype(out[name].dtype)
    return out
```

```python
from contextlib import ExitStack

import concourse.bass as bass
import numpy as np
from concourse import mybir

F32 = mybir.dt.float32
F16 = mybir.dt.float16
BF16 = mybir.dt.bfloat16
ALU = mybir.AluOpType
ACT = mybir.ActivationFunctionType
AX_X = mybir.AxisListType.X

B, HW, C = 32, 56, 32
HEADS, EXPERTS = 16, 8
PR = HW // 2
G = 4
TILES = 7
YL = PR // TILES
PT = YL * PR
SLOTS = TILES * G
PATCHES = TILES * PT
TOKENS = HW * HW
DH = HEADS * C
CH = DH // 128
HPC = HEADS // CH
PITCH = PR + 2
HALF = (4, 3)
COL = [(0, 4 * PT), (4 * PT, 7 * PT)]
LN_EPS, GN_EPS, BN_EPS = 1e-5, 1e-5, 1e-3
DEN_EPS = 1e-5
SHIFT = 2.0 ** -22


def consts():
    eye = np.eye(128, dtype=np.float32)
    i32 = np.eye(32, dtype=np.float32)
    center = np.kron(np.eye(4), i32 - 1.0 / 32).astype(np.float32)
    mean4 = np.kron(np.ones((4, 4)), i32 / 4).astype(np.float32)
    pair = np.concatenate([np.kron(np.eye(2), np.kron(np.ones((2, 1)), m))
                           for m in (i32, i32 - 1.0 / 32)], 1).astype(np.float32)
    dsum = np.kron(np.eye(4), np.kron(np.ones((2, 1)), np.eye(16)))
    dsum = np.concatenate([dsum, dsum], 1).astype(np.float32)
    sel = np.zeros((2, G, HEADS, CH, G, HPC, 32), np.float32)
    for g in range(G):
        for h in range(HEADS):
            sel[:, g, h, h // HPC, g, h % HPC, :] = 1.0
    p2 = np.zeros((2, 2, 32, CH, 2, HPC, 33), np.float32)
    for cs in range(2):
        p2[:, cs, 31, :, cs, :, 32] = SHIFT
    tile, g, yl, px = np.meshgrid(np.arange(TILES), np.arange(G), np.arange(YL), np.arange(PR), indexing="ij")
    row, col = 2 * (TILES * yl + tile) + g // 2, 2 * px + g % 2
    s = (row * HW + col).reshape(TILES, G, PT)
    pos = np.float32(1.57) * np.arange(TOKENS, dtype=np.float32) / np.float32(TOKENS)
    cs = np.stack([np.cos(pos), np.sin(pos)]).astype(np.float32)[:, s]
    tabd = np.repeat(cs.transpose(2, 0, 1, 3)[:, :, None], HEADS, 2).reshape(128, PATCHES)
    v = cs.reshape(2, TILES, 2, 2, PT)
    tabn = np.repeat(v.transpose(3, 0, 1, 2, 4)[:, :, None], 32, 2).reshape(128, 2 * PATCHES)
    tabk = cs.transpose(3, 0, 1, 2).reshape(PT, 2 * SLOTS)
    first = np.tile(np.arange(EXPERTS, 0, -1, dtype=np.float32), (PT, SLOTS))
    valid = np.zeros((G, 32, 2, 2, G, 32), np.float32)
    for (di, dj, gi, i, j, go) in _taps():
        valid[gi, :, i, j, go, :] = 1.0
    return dict(eyec=np.concatenate([eye, center], 1), mean4=mean4, pair=pair, dsum=dsum,
                sel=sel.reshape(128, -1), p2=p2.reshape(128, -1), tabd=tabd, tabn=tabn, tabk=tabk,
                first=first, valid=valid.reshape(128, -1))


def _taps():
    for gi in range(G):
        for go in range(G):
            for i in range(2):
                for j in range(2):
                    kh = 2 * i + 1 - gi // 2 - go // 2
                    kw = 2 * j + 1 - gi % 2 - go % 2
                    if 0 <= kh <= 2 and 0 <= kw <= 2:
                        yield kh, kw, gi, i, j, go


class Img:

    def __init__(self, t, c):
        self.t, self.c = t, c

    def at(self, per, off=0):
        return self.c * per + off if self.t is None else self.t * (2 * per) + (self.c * per + off)

    @property
    def par(self):
        return self.c % 2


RING = {"K": 14, "R": 14, "Q": 14, "G": 2, "LG": 1, "F": 7}
MISC = {"XT": 2, "CV": 2, "XC": 2, "ZT": 4, "SU": 2, "T2": 4, "ZU": 4}


def plan(prev, cur, nxt):
    out = []

    def add(kind, d, n=0):
        if {-1: prev, 0: cur, 1: nxt}[d]:
            out.append((kind, d, n))

    for n in range(14):
        add("K", 0, n)
        if n:
            add("KX", 0, n - 1)
        add("R", -1, n)
        if n in (4, 8, 12):
            add("NM", -1, n // 4 - 1)
        if n in (6, 10):
            add("T2", -1, (n - 6) // 4)
        if n in (4, 5):
            add("XT", 1, n - 4)
        if n in (8, 9):
            add("CV", 1, n - 8)
        if n in (11, 12):
            add("XC", 1, n - 11)
        if n == 13:
            add("SM1", 1)
            add("PN1", 1)
    add("KX", 0, 13)
    add("NM", -1, 3)
    add("KT", 0)
    add("T2", -1, 2)
    add("G", 0, 0)
    add("T2", -1, 3)
    add("G", 0, 1)
    add("SM2", -1)
    add("PN2", -1)
    add("TB", 0)
    for n in range(14):
        add("Q", 0, n)
        if n and n % 2 == 0:
            add("DN", 0, n // 2 - 1)
        if n == 0:
            add("XH1", 1)
            add("PL1", 1)
        if n == 2:
            add("XH2", -1)
            add("PL2", -1)
            add("CS", 1)
        if 2 <= n < 6:
            add("ZT", 1, n - 2)
        if 6 <= n < 10:
            add("ZU", -1, n - 6)
        if n == 10:
            add("LG", -1)
            add("SU", 0, 0)
            add("RC", 0, 0)
        if n >= 12:
            add("F", -1, n - 12)
    add("DN", 0, 6)
    add("F", -1, 2)
    add("SU", 0, 1)
    add("RC", 0, 1)
    for n in range(3, 7):
        add("F", -1, n)
    add("OUT", -1)
    return out


PRELUDE = [("XT", 0), ("XT", 1), ("CV", 0), ("CV", 1), ("XC", 0), ("XC", 1), ("SM1", 0), ("PN1", 0), ("XH1", 0),
           ("PL1", 0), ("CS", 0), ("ZT", 0), ("ZT", 1), ("ZT", 2), ("ZT", 3)]


def walk(eng, step):
    def run(steps, t, i):
        done = []
        for kind, d, n in steps:
            m = Img(t, i + d)
            step(kind, m, n, done, Img(t, i))
            done.append((kind, m, n))

    run([(k, 1, n) for k, n in PRELUDE], None, -1)
    run(plan(False, True, True), None, 0)
    run(plan(True, True, True), None, 1)
    with eng.Fori(0, (B - 4) // 2) as t:
        run(plan(True, True, True), t, 2)
        run(plan(True, True, True), t, 3)
    run(plan(True, True, True), None, B - 2)
    run(plan(True, True, False), None, B - 1)
    run(plan(True, False, False), None, B)


def build(nc, x, gamma, beta, conv_taps, conv_rows, wq, wk, wv, wd, wd_b, we, eyec, mean4, pair, dsum, sel,
          p2c, tabdc, tabnc, tabkc, firstc, validc, out):
    ctx = ExitStack()
    with ctx:
        def sb(name, shape, dt=F32):
            return ctx.enter_context(nc.sbuf_tensor(name, shape, dt))

        def sem(name):
            return ctx.enter_context(nc.semaphore(name))

        eye_center = sb("eye_center", [128, 256])
        mean4_sb = sb("mean4_sb", [128, 128])
        pair_sb = sb("pair_sb", [128, 128])
        dsum_sb = sb("dsum_sb", [128, 128])
        eye16 = sb("eye16", [128, 128], F16)
        sel16 = sb("sel16", [128, CH * G * 128], F16)
        p2 = sb("p2", [128, CH, 2, HPC, 33])
        tabd = sb("tabd", [128, PATCHES])
        tabn = sb("tabn", [128, TILES, 2 * PT])
        tabk = sb("tabk", [PT, 2, SLOTS])
        first = sb("first", [PT, SLOTS * EXPERTS])
        conv_w = sb("conv_w", [128, 4, 128], BF16)
        wq16 = sb("wq16", [128, DH], F16)
        wk16 = sb("wk16", [128, DH], F16)
        we16 = sb("we16", [128, EXPERTS * C + EXPERTS], F16)
        small = sb("small", [128, 16])
        gamma_c, beta_c, dense_b = (small[:, k:k + 1] for k in range(3))
        conv_scale, conv_sum, conv_bias, conv_scale2 = (small[:, k:k + 1] for k in range(3, 7))
        minus_one, den_eps, bn_inv, bn_half = (small[:, k:k + 1] for k in range(7, 11))
        bn_gain = small[:, 11:12]
        bin_a = sb("bin_a", [128, B])
        bin_thr = sb("bin_thr", [128, B])
        power = sb("power", [128, B])
        xt = sb("xt", [PT, TILES * G * C])
        nat = sb("nat", [128, PITCH, PITCH], BF16)
        shifted = sb("shifted", [128, PITCH, PITCH], BF16)
        xres = sb("xres", [128, PATCHES])
        t1 = sb("t1", [128, 2, PATCHES])
        t1b = sb("t1b", [128, PATCHES])
        xc = [sb(f"xc{k}", [PT, SLOTS, C]) for k in (1, 2)]
        sq = [sb(f"sq{k}", [PT, SLOTS, C]) for k in (1, 2)]
        xn = [sb(f"xn{k}", [PT, SLOTS, C]) for k in (1, 2)]
        parts = [sb(f"parts{k}", [PT, SLOTS, 2 * C], F16) for k in (1, 2)]
        ssum = [sb(f"ssum{k}", [PT, SLOTS]) for k in (1, 2)]
        varr = [sb(f"varr{k}", [PT, SLOTS]) for k in (1, 2)]
        rstd = [sb(f"rstd{k}", [PT, SLOTS]) for k in (1, 2)]
        xcs = sb("xcs", [PT, SLOTS, 2, C])
        z1 = sb("z1", [128, 2, SLOTS * PT], F16)
        z2 = sb("z2", [128, SLOTS * PT], F16)
        ebuf = sb("ebuf", [128, 2, 1024])
        kbuf = sb("kbuf", [PT, 2, 1024])
        ktsb = sb("ktsb", [128, DH])
        gmat = sb("gmat", [128, CH, 2, C])
        dmat = sb("dmat", [128, CH, 2, HEADS])
        qbuf = sb("qbuf", [128, CH, TILES, G * PT])
        dcs = sb("dcs", [128, PATCHES])
        den = sb("den", [128, PATCHES])
        rs = sb("rs", [128, PATCHES], F16)
        pbuf = sb("pbuf", [128, TILES, 2, PT])
        t2 = sb("t2", [PT, TILES * G * C])
        route = sb("route", [PT, 4, SLOTS * EXPERTS])
        rmax = sb("rmax", [PT, 6, SLOTS])
        gate = sb("gate", [PT, SLOTS * EXPERTS])
        prod = sb("prod", [PT, 2, 4, EXPERTS * C])
        half1 = sb("half1", [PT, 4, 4 * C])
        half2 = sb("half2", [PT, 4, 2 * C])
        ffn = sb("ffn", [PT, SLOTS, C])
        qflat = qbuf[:, :, :, :].rearrange("p a b c -> p (a b c)")
        stage = [qflat[0:PT, k * 3584:(k + 1) * 3584].rearrange("p (b f) -> p b f", b=4) for k in range(2)]
        at, views = 2 * 3584, {}
        for name, width in (("taps", 512), ("valid", 512), ("rows", 288), ("rows2", 288), ("wqa", DH), ("wka", DH),
                            ("wea", 264), ("tmp", 512)):
            views[name] = qflat[:, at:at + width]
            at += width
        assert at <= CH * TILES * G * PT
        wqb_s, wkb_s, web_s = ebuf[:, 0, 0:DH], ebuf[:, 0, DH:2 * DH], ebuf[:, 1, 0:264]
        wva_s, wvb_s = t1[0:32, 0, 0:DH], t1[0:32, 1, 0:DH]
        wd_s = t1b[0:32, 0:DH]
        sel_s = [pbuf[:, :, :, :].rearrange("p a b c -> p (a b c)")[:, 0:1024], tabn]
        wvr = xres[0:32, 0:128]
        stats = dcs[:, 0:B * 12].rearrange("p (b k) -> p b k", b=B)
        mv = den[:, 0:B * 2].rearrange("p (b k) -> p b k", b=B)
        bw = den[:, 64:64 + 8 * B].rearrange("p (k b) -> p k b", k=8)

        ps = ctx.enter_context(nc.psum_tensor("ps", [128, 8, 512], F32))

        def ring(s):
            return ps[:, 2 * s:2 * s + 2, :]

        def misc(s):
            return ps[:, 4 + s, :]

        kt_bank = ps[:, 6, :]
        nd_bank = ps[:, 7, :]

        consts_in = sem("consts_in")
        eye_in = sem("eye_in")
        stage_in = [sem(f"stage_in{k}") for k in range(2)]
        stage_turned = sem("stage_turned")
        stage_read = sem("stage_read")
        pe_pre = sem("pe_pre")
        eye16_made = sem("eye16_made")
        dve_pre = sem("dve_pre")
        pool_pre = sem("pool_pre")
        act_pre = sem("act_pre")
        x_in = sem("x_in")
        shift_in = sem("shift_in")
        out_stored = sem("out_stored")
        ring_full = sem("ring_full")
        misc_full = sem("misc_full")
        nd_full = sem("nd_full")
        nd_read = sem("nd_read")
        binarized = sem("binarized")
        xres_made = sem("xres_made")
        t1_made = sem("t1_made")
        xc_made = [sem(f"xc_made{k}") for k in (1, 2)]
        ssum_made = [sem(f"ssum_made{k}") for k in (1, 2)]
        var_made = [sem(f"var_made{k}") for k in (1, 2)]
        rstd_made = [sem(f"rstd_made{k}") for k in (1, 2)]
        xn_made = [sem(f"xn_made{k}") for k in (1, 2)]
        high_made = [sem(f"high_made{k}") for k in (1, 2)]
        parts_made = [sem(f"parts_made{k}") for k in (1, 2)]
        z_made = [sem(f"z_made{k}") for k in (1, 2)]
        xcs_made = sem("xcs_made")
        kexp_made = sem("kexp_made")
        qexp_made = sem("qexp_made")
        k_made = sem("k_made")
        q_made = sem("q_made")
        ktx_done = sem("ktx_done")
        kt_copied = sem("kt_copied")
        g_made = sem("g_made")
        den_made = sem("den_made")
        recip_made = sem("recip_made")
        rhigh_made = sem("rhigh_made")
        r_made = sem("r_made")
        qr_made = sem("qr_made")
        t1b_made = sem("t1b_made")
        t2_made = sem("t2_made")
        route_step = sem("route_step")
        ratio_made = sem("ratio_made")
        gate_made = sem("gate_made")
        prod_made = sem("prod_made")
        pool_add = sem("pool_add")
        ffn_made = sem("ffn_made")
        out_made = sem("out_made")

        def wait(eng, s, v):
            if not isinstance(v, int) or v > 0:
                eng.wait_ge(s, v)

        def ring_no(done, it):
            n = sum(k in RING for k, _, _ in done)
            if it.t is None and it.c <= 0:
                return n % 2, n
            return n % 2, it.at(52, n - 22)

        def misc_no(done, it):
            n = sum(k in MISC for k, _, _ in done)
            if it.t is None and it.c <= 0:
                base = 0 if it.c < 0 else 10
                return n % 2, n + base
            return n % 2, it.at(20, n + (2 if it.t is not None or it.c < B else -8))

        def nd_no(done, it):
            n = sum(k == "NM" or (k == "DN" and j in (3, 6)) for k, _, j in done)
            return n if it.t is None and it.c == 0 else it.at(6, n - 4)

        READ = {"K": (k_made, 14), "R": (qr_made, 14), "Q": (q_made, 14), "G": (g_made, 2), "LG": (route_step, 18),
                "F": (prod_made, 7), "XT": (xres_made, 2), "CV": (t1_made, 2), "XC": (xc_made[0], 2),
                "ZT": (z_made[0], 4), "SU": (den_made, 2), "T2": (t2_made, 4), "ZU": (z_made[1], 4)}

        block = ctx.enter_context(nc.Block())

        @block.sync
        def _(sp):
            sp.dma_start(eye_center[:, :], eyec).then_inc(eye_in, 16)
            for dst, src in ((mean4_sb[:, :], mean4), (views["rows"], conv_rows),
                             (small[:, 0:1], gamma), (small[:, 1:2], beta), (small[:, 2:3], wd_b)):
                sp.dma_start(dst, src).then_inc(consts_in, 16)
            x4 = x.rearrange("(q b) h w c -> q b (h w c)", b=4).rearrange("q b (p f) -> q p b f", p=PT)

            def stage_load(q, k, turned):
                wait(sp, stage_turned, turned)
                sp.dma_start(stage[k], q).then_inc(stage_in[k], 16)

            for k in range(2):
                stage_load(x4[k], k, 0)
            for dst, src in ((pair_sb[:, :], pair), (dsum_sb[:, :], dsum), (views["taps"], conv_taps),
                             (views["valid"], validc), (views["wqa"], wq[0]), (wqb_s, wq[1]), (views["wka"], wk[0]),
                             (wkb_s, wk[1]), (views["wea"], we[0]), (web_s, we[1]), (wva_s, wv[0]), (wvb_s, wv[1]),
                             (wd_s, wd), (p2[:, :, :, :, :].rearrange("p a b c d -> p (a b c d)"), p2c),
                             (tabd[:, :], tabdc), (tabk[:, :, :].rearrange("p a b -> p (a b)"), tabkc),
                             (first[:, :], firstc), (sel_s[0], sel[:, 0:1024]),
                             (qflat[:, at:at + 1024], sel[:, 1024:2048]),
                             (tabn[:, :, :].rearrange("p a b -> p (a b)"), tabnc)):
                sp.dma_start(dst, src).then_inc(consts_in, 16)
            with sp.Fori(1, 4) as t:
                for k in range(2):
                    wait(sp, stage_turned, t * 8 + (4 * k - 4))
                    sp.dma_start(stage[k], x4[bass.ds(t * 2 + k, 1)].rearrange("q p b f -> (q p) b f"))\
                        .then_inc(stage_in[k], 16)

            xt_v = xt[:, :].rearrange("p (j d e) -> p j d e", j=TILES, d=2)

            def rows_of(a, m, yl):
                img = a[m.at(1):m.at(1) + 1] if m.t is None else a[bass.ds(m.at(1), 1)]
                return img.rearrange("b (q j d) (z e) c -> (b q) z (j d) (e c)", j=TILES, d=2, e=2)[yl]

            def load(m):
                for yl in range(YL):
                    sp.dma_start(xt_v[PR * yl:PR * yl + PR].rearrange("p j d e -> p (j d) e"), rows_of(x, m, yl))\
                        .then_inc(x_in, 16)

            def step(kind, m, n, done, it):
                if kind == "XT" and n == 0:
                    wait(sp, xres_made, m.at(2))
                    load(m)
                if kind == "CV" and n == 0:
                    sp.wait_ge(binarized, m.at(2, 2))
                    wait(sp, t1_made, m.at(2))
                    for g in range(G):
                        dy, dx = g // 2, g % 2
                        q = slice(32 * g, 32 * g + 32)
                        src = nat[q, 1 - dy:1 - dy + PR + 1, 1 - dx:1 - dx + PR + 1]
                        sp.dma_start(shifted[q, 0:PR + 1, 0:PR + 1], src).then_inc(shift_in, 16)
                if kind == "OUT":
                    sp.wait_ge(out_made, m.at(1, 1))
                    for yl in range(YL):
                        src = ffn[PR * yl:PR * yl + PR, :, :].rearrange("p (a e) c -> p a (e c)", e=2)
                        sp.dma_start(rows_of(out, m, yl), src).then_inc(out_stored, 16)

            walk(sp, step)
            sp.wait_ge(out_stored, 16 * YL * B)

        @block.tensor
        def _(pe):
            eye = eye_center[:, 0:128]
            pe.wait_ge(eye_in, 16)
            def turn(t):
                for k in range(2):
                    pe.wait_ge(stage_in[k], t * 16 + 16)
                    for b in range(4):
                        wait(pe, stage_read, t * 8 + (4 * k + b - 3))
                        for j in range(TILES):
                            bank = 2 * b + (j >= 4)
                            dst = ps[:, bank, (j % 4) * PT:(j % 4 + 1) * PT]
                            mm = pe.transpose(dst, stage[k][:, b, j * 128:(j + 1) * 128], eye[0:PT, 0:PT])
                        mm.then_inc(stage_turned, 1)

            turn(0)
            with pe.Fori(1, 4) as t:
                turn(t)
            pe.wait_ge(consts_in, 16 * 25)
            pe.wait_ge(dve_pre, 1)
            pe.matmul(ps[:, 0, 0:B], mean4_sb[:, :], bw[:, 0, :], start=True, stop=True).then_inc(pe_pre, 1)
            pe.wait_ge(dve_pre, 2)
            pe.matmul(ps[:, 1, 0:B], mean4_sb[:, :], bw[:, 2, :], start=True, stop=True).then_inc(pe_pre, 1)
            for h in range(HEADS):
                pe.wait_ge(dve_pre, 3 + h)
                mm = pe.matmul(ps[:, 2, C * h:C * h + C], wvr[:, :] if h % 2 == 0 else xres[0:32, 128:256],
                               wd_s[:, C * h:C * h + C], start=True, stop=True)
                mm.then_inc(pe_pre, 1)

            def slot_free(kinds, done, it):
                past = [(k, m, n) for k, m, n in done if k in kinds]
                if len(past) >= 2:
                    k, m, n = past[-2]
                    s, per = READ[k]
                    pe.wait_ge(s, m.at(per, n + 1))
                elif kinds is RING:
                    wait(pe, q_made, it.at(14))
                    wait(pe, prod_made, it.at(7, -7))
                else:
                    wait(pe, den_made, it.at(2))
                    wait(pe, z_made[0], it.at(4, 4) if it.t is not None or it.c < B else 4 * B)
                    wait(pe, z_made[1], it.at(4, -4))

            def nd_free(done, it):
                wait(pe, nd_read, nd_no(done, it))

            def step(kind, m, n, done, it):
                if kind in RING:
                    slot_free(RING, done, it)
                    o = ring(ring_no(done, it)[0])
                if kind in MISC:
                    slot_free(MISC, done, it)
                    o = misc(misc_no(done, it)[0])
                if kind == "XT":
                    pe.wait_ge(x_in, m.at(64, 64))
                    for k in range(HALF[n]):
                        j = 4 * n + k
                        mm = pe.transpose(o[:, PT * k:PT * k + PT], xt[:, 128 * j:128 * j + 128], eye[0:PT, 0:PT])
                    mm.then_inc(misc_full, 1)
                elif kind == "CV":
                    pe.wait_ge(shift_in, m.at(64, 64))
                    w = HALF[n]
                    dst = o[:, 0:w * PT].rearrange("p (j y x) -> p j y x", j=w, y=YL)
                    for k in range(4):
                        di, dj = k // 2, k % 2
                        src = shifted[:, di:di + PR, dj:dj + PR].rearrange("p (y j) x -> p j y x", j=TILES)
                        mm = pe.matmul(dst, conv_w[:, k, :], src[:, 4 * n:4 * n + w], start=(k == 0), stop=(k == 3))
                    mm.then_inc(misc_full, 1)
                elif kind == "XC":
                    pe.wait_ge(t1_made, m.at(2, n + 1))
                    for k in range(HALF[n]):
                        j = 4 * n + k
                        mm = pe.matmul(o[0:PT, 128 * k:128 * k + 128], t1[:, m.par, PT * j:PT * j + PT],
                                       eye_center[:, 128:256], start=True, stop=True)
                    mm.then_inc(misc_full, 1)
                elif kind in ("ZT", "ZU"):
                    ln = kind == "ZU"
                    pe.wait_ge(parts_made[ln], m.at(1, 1))
                    pe.wait_ge(eye16_made, 1)
                    of = o.bitcast(F16)
                    for k in range(7):
                        for q, w in (((0, 32), (32, 32), (64, 32), (96, 32)) if k == 0 else ((0, 64), (64, 64))):
                            mm = pe.matmul(of[q:q + w, PT * k:PT * k + PT], parts[ln][:, 7 * n + k, q % 64:q % 64 + w],
                                           eye16[0:PT, 0:PT], is_transpose=True, start=True, stop=True)
                    mm.then_inc(misc_full, 1)
                elif kind == "K":
                    pe.wait_ge(z_made[0], m.at(4, (2 * n + 1) // 7 + 1))
                    for k in range(2):
                        s = 2 * n + k
                        mm = pe.matmul(o[0:PT, k, :], z1[:, m.par, PT * s:PT * s + PT], wk16[:, :], start=True, stop=True)
                    mm.then_inc(ring_full, 1)
                elif kind == "KX":
                    pe.wait_ge(k_made, m.at(14, n + 1))
                    if n == 0:
                        pe.wait_ge(xcs_made, m.at(1, 1))
                        wait(pe, kt_copied, m.at(1))
                    for k in range(2):
                        mm = pe.matmul(kt_bank[64 * k:64 * k + 64, :],
                                       xcs[:, 2 * n + k, :, :].rearrange("p a c -> p (a c)"),
                                       kbuf[:, n % 2, DH * k:DH * k + DH], start=(n == 0), stop=(n == 13))
                    mm.then_inc(ktx_done, 1)
                elif kind == "G":
                    pe.wait_ge(kt_copied, m.at(1, 1))
                    for k in range(2):
                        c = 2 * n + k
                        mm = pe.matmul(o[:, k, 0:2 * HPC * 33], ktsb[:, 128 * c:128 * c + 128],
                                       p2[:, c, :, :, :].rearrange("p a h o -> p (a h o)"), start=True, stop=True)
                    mm.then_inc(ring_full, 1)
                elif kind == "Q":
                    j, k0 = n // 2, 2 * (n % 2)
                    for k in range(2):
                        mm = pe.matmul(o[:, k, 0:G * PT], wq16[:, 128 * (k0 + k):128 * (k0 + k) + 128],
                                       z1[:, m.par, G * PT * j:G * PT * (j + 1)], start=True, stop=True)
                    mm.then_inc(ring_full, 1)
                elif kind == "DN":
                    pe.wait_ge(q_made, m.at(14, 2 * n + 2))
                    if n == 0:
                        pe.wait_ge(g_made, m.at(2, 2))
                    if n in (0, 4):
                        nd_free(done, it)
                    k = n % 4
                    for c in range(CH):
                        for g in range(G):
                            mm = pe.matmul(nd_bank[32 * g:32 * g + 32, PT * k:PT * k + PT],
                                           dmat[:, c, :, :].rearrange("p a h -> p (a h)"),
                                           qbuf[:, c, n, PT * g:PT * g + PT], start=(c == 0), stop=(c == CH - 1))
                    if n in (3, 6):
                        mm.then_inc(nd_full, 1)
                elif kind == "SU":
                    pe.wait_ge(nd_read, nd_count(done, it))
                    a, b = COL[n]
                    pe.matmul(o[:, 0:b - a], dsum_sb[:, :], dcs[:, a:b], start=True, stop=True).then_inc(misc_full, 1)
                elif kind == "R":
                    j, k0 = n // 2, 2 * (n % 2)
                    pe.wait_ge(r_made, m.at(2, 1 + (j >= 4)))
                    for k in range(2):
                        for g in range(G):
                            c = k0 + k
                            mm = pe.matmul(o[:, k, PT * g:PT * g + PT], sel16[:, 128 * (G * c + g):128 * (G * c + g) + 128],
                                           rs[:, PT * j:PT * j + PT], start=True, stop=True)
                    mm.then_inc(ring_full, 1)
                elif kind == "NM":
                    tiles = range(2 * n, min(2 * n + 2, TILES))
                    pe.wait_ge(qr_made, m.at(14, 2 * tiles[-1] + 2))
                    nd_free(done, it)
                    for jj, j in enumerate(tiles):
                        for c in range(CH):
                            for v in range(2):
                                rhs = qbuf[:, c, j, :].rearrange("p (a v t) -> p a v t", a=2, v=2)[:, :, v, :]
                                dst = nd_bank[64 * v:64 * v + 64, 2 * PT * jj:2 * PT * jj + 2 * PT]
                                mm = pe.matmul(dst.rearrange("p (a t) -> p a t", a=2),
                                               gmat[:, c, :, :].rearrange("p a o -> p (a o)"), rhs,
                                               start=(c == 0), stop=(c == CH - 1))
                    mm.then_inc(nd_full, 1)
                elif kind == "T2":
                    tiles = range(2 * n, min(2 * n + 2, TILES))
                    pe.wait_ge(nd_read, nd_count(done, it, n))
                    if n == 0:
                        pe.wait_ge(t1b_made, m.at(1, 1))
                    for jj, j in enumerate(tiles):
                        dst = o[0:PT, 256 * jj:256 * jj + 256]
                        pe.matmul(dst, t1b[:, PT * j:PT * j + PT], eye_center[:, :], start=True, stop=False)
                        for a in range(2):
                            mm = pe.matmul(dst.rearrange("p (q a c) -> p q a c", q=2, a=2)[:, :, a, :],
                                           pbuf[:, j, a, :], pair_sb[:, :].rearrange("p (q c) -> p q c", q=2),
                                           start=False, stop=(a == 1))
                    mm.then_inc(misc_full, 1)
                elif kind == "LG":
                    pe.wait_ge(z_made[1], m.at(4, 4))
                    for s in range(SLOTS):
                        mm = pe.matmul(o[0:PT, 0, EXPERTS * s:EXPERTS * s + EXPERTS], z2[:, PT * s:PT * s + PT],
                                       we16[:, EXPERTS * C:], start=True, stop=True)
                    mm.then_inc(ring_full, 1)
                elif kind == "F":
                    for k in range(4):
                        s = 4 * n + k
                        mm = pe.matmul(o[0:PT, k // 2, 256 * (k % 2):256 * (k % 2) + 256], z2[:, PT * s:PT * s + PT],
                                       we16[:, 0:EXPERTS * C], start=True, stop=True)
                    mm.then_inc(ring_full, 1)

            def nd_count(done, it, t2_round=None):
                if t2_round is None:
                    return nd_no(done, it)
                upto = [d for k, d in enumerate(done) if d[0] != "NM" or d[2] <= t2_round]
                return nd_no(upto, it)

            pe.wait_ge(dve_pre, 22)
            walk(pe, step)

        @block.scalar
        def _(act):
            act.wait_ge(dve_pre, 19)
            for v in range(2):
                for cs in range(2):
                    q = slice(64 * v + 32 * cs, 64 * v + 32 * cs + 32)
                    dst = p2[q, :, cs, :, 0:C]
                    last = act.activation(dst, ps[q, 2, :].rearrange("p (a h o) -> p a h o", a=CH, h=HPC), ACT.Copy,
                                          scale=SHIFT)
            last.then_inc(act_pre, 1)
            act.wait_ge(dve_pre, 22)

            def step(kind, m, n, done, it):
                if kind in RING:
                    s, no = ring_no(done, it)
                    o = ring(s)
                if kind in MISC:
                    s, no = misc_no(done, it)
                    o = misc(s)
                if kind == "XT":
                    act.wait_ge(binarized, m.at(2, n + 1))
                    if n == 0:
                        wait(act, t1_made, m.at(2))
                    a, b = COL[n]
                    act.activation(xres[:, a:b], o[:, 0:b - a], ACT.Identity, bias=conv_bias).then_inc(xres_made, 1)
                elif kind == "XC":
                    act.wait_ge(misc_full, no + 1)
                    if n == 0:
                        wait(act, parts_made[0], m.at(1))
                        wait(act, ssum_made[0], m.at(1))
                    a, w = 16 * n, 4 * HALF[n]
                    src = o[0:PT, 0:w * C].rearrange("p (s c) -> p s c", c=C)
                    act.activation(xc[0][:, a:a + w, :], src, ACT.Copy)
                    act.activation(sq[0][:, a:a + w, :], src, ACT.Square).then_inc(xc_made[0], 1)
                elif kind in ("XH1", "XH2"):
                    ln = kind == "XH2"
                    act.wait_ge(xn_made[ln], m.at(1, 1))
                    act.activation(parts[ln][:, :, 0:C], xn[ln][:, :, :], ACT.Copy).then_inc(high_made[ln], 1)
                elif kind in ("ZT", "ZU"):
                    ln = kind == "ZU"
                    act.wait_ge(misc_full, no + 1)
                    if ln and n == 0:
                        wait(act, prod_made, m.at(7))
                    dst = (z2 if ln else z1[:, m.par, :])[:, 7 * PT * n:7 * PT * (n + 1)]
                    act.activation(dst, o.bitcast(F16)[:, 0:7 * PT], ACT.Copy).then_inc(z_made[ln], 1)
                elif kind == "K":
                    act.wait_ge(ring_full, no + 1)
                    if n < 2:
                        wait(act, q_made, m.at(14))
                    else:
                        act.wait_ge(k_made, m.at(14, n - 1))
                    act.activation(ebuf[0:PT, n % 2, :].rearrange("p (a b) -> p a b", a=2), o[0:PT, :, :], ACT.Exp,
                                   bias=minus_one[0:PT, :]).then_inc(kexp_made, 1)
                elif kind == "Q":
                    act.wait_ge(ring_full, no + 1)
                    act.wait_ge(k_made, m.at(14, 14)) if n < 2 else act.wait_ge(q_made, m.at(14, n - 1))
                    act.activation(ebuf[:, n % 2, 0:2 * G * PT].rearrange("p (a b) -> p a b", a=2), o[:, :, 0:G * PT],
                                   ACT.Exp, bias=minus_one).then_inc(qexp_made, 1)
                elif kind == "KT":
                    act.wait_ge(ktx_done, m.at(14, 14))
                    act.activation(ktsb[:, :], kt_bank, ACT.Copy).then_inc(kt_copied, 1)
                elif kind == "G":
                    act.wait_ge(ring_full, no + 1)
                    src = o[:, :, 0:2 * HPC * 33].rearrange("p k (a h o) -> p k a h o", a=2, h=HPC)
                    dflat = dmat[:, :, :, :].rearrange("p c a h -> p (c a h)")
                    for h in range(HPC):
                        q = slice(32 * h, 32 * h + 32)
                        act.activation(gmat[q, 2 * n:2 * n + 2, :, :], src[q, :, :, h, 0:C], ACT.Copy)
                        for k in range(2):
                            c = 2 * n + k
                            last = act.activation(dmat[q, c, :, HPC * c + h], src[q, k, :, h, C], ACT.Copy)
                    last.then_inc(g_made, 1)
                elif kind == "SU":
                    act.wait_ge(misc_full, no + 1)
                    wait(act, r_made, m.at(2, n)) if n == 0 else None
                    a, b = COL[n]
                    act.activation(den[:, a:b], o[:, 0:b - a], ACT.Identity, bias=den_eps).then_inc(den_made, 1)
                elif kind == "T2":
                    act.wait_ge(misc_full, no + 1)
                    if n == 0:
                        wait(act, out_made, m.at(1))
                        wait(act, parts_made[1], m.at(1))
                        wait(act, ssum_made[1], m.at(1))
                    w = min(2, TILES - 2 * n)
                    src = o[0:PT, 0:256 * w].rearrange("p (j q f) -> p j q f", j=w, q=2)
                    cen = src[:, :, 1, :].rearrange("p j (g c) -> p j g c", g=G)
                    a = 2 * n
                    act.activation(t2[:, 128 * a:128 * (a + w)].rearrange("p (j f) -> p j f", j=w), src[:, :, 0, :],
                                   ACT.Copy)
                    sl = slice(G * a, G * (a + w))
                    act.activation(xc[1][:, sl, :].rearrange("p (j g) c -> p j g c", j=w), cen, ACT.Copy)
                    act.activation(sq[1][:, sl, :].rearrange("p (j g) c -> p j g c", j=w), cen, ACT.Square)\
                        .then_inc(t2_made, 1)
                elif kind == "TB":
                    act.wait_ge(t1_made, m.at(2, 2))
                    act.activation(t1b[:, :], t1[:, m.par, :], ACT.Identity, bias=dense_b).then_inc(t1b_made, 1)
                elif kind == "LG":
                    act.wait_ge(route_step, m.at(18, 13))
                    act.activation(rmax[:, 3, :], rmax[:, 2, :], ACT.Exp).then_inc(ratio_made, 1)

            walk(act, step)

        @block.gpsimd
        def _(pool):
            nc.gpsimd.memset(power[:, :], -0.5).then_inc(pool_pre, 1)
            pool.wait_ge(pool_pre, 1)
            pool.wait_ge(dve_pre, 20)
            nc.gpsimd.tensor_tensor(bw[:, 4, :], bw[:, 3, :], power[:, :], ALU.pow).then_inc(pool_pre, 1)
            pool.wait_ge(dve_pre, 21)
            nc.gpsimd.tensor_tensor(bn_inv, bn_half, power[:, 0:1], ALU.pow).then_inc(pool_pre, 1)

            def step(kind, m, n, done, it):
                if kind in ("PN1", "PN2"):
                    ln = kind == "PN2"
                    pool.wait_ge(var_made[ln], m.at(1, 1))
                    nc.gpsimd.tensor_tensor(rstd[ln][:, :], varr[ln][:, :], power[0:PT, 0:SLOTS], ALU.pow)\
                        .then_inc(rstd_made[ln], 1)
                    pool.wait_ge(rstd_made[ln], m.at(1, 1))
                    wait(pool, high_made[ln], m.at(1))
                    nc.gpsimd.tensor_tensor(xn[ln][:, :, 0:C - 1], xc[ln][:, :, 0:C - 1],
                                            rstd[ln][:, :].unsqueeze(2).to_broadcast([PT, SLOTS, C - 1]), ALU.mult)\
                        .then_inc(xn_made[ln], 1)
                elif kind in ("PL1", "PL2"):
                    ln = kind == "PL2"
                    pool.wait_ge(high_made[ln], m.at(1, 1))
                    nc.gpsimd.tensor_tensor(parts[ln][:, :, C:2 * C], xn[ln][:, :, :], parts[ln][:, :, 0:C],
                                            ALU.subtract).then_inc(parts_made[ln], 1)
                elif kind == "CS":
                    pool.wait_ge(xn_made[0], m.at(1, 1))
                    wait(pool, ktx_done, m.at(14))
                    for k in range(2):
                        last = nc.gpsimd.tensor_tensor(xcs[:, :, k, :], xn[0][:, :, :],
                                                       tabk[:, k, :].unsqueeze(2).to_broadcast([PT, SLOTS, C]), ALU.mult)
                    last.then_inc(xcs_made, 1)
                elif kind == "F":
                    pool.wait_ge(prod_made, m.at(7, n + 1))
                    if n == 0:
                        wait(pool, out_stored, m.at(64))
                    p = prod[:, n % 2, :, :]
                    nc.gpsimd.tensor_tensor(half1[:, :, :], p[:, :, 0:4 * C], p[:, :, 4 * C:], ALU.add)\
                        .then_inc(pool_add, 1)
                    pool.wait_ge(pool_add, m.at(14, 2 * n + 1))
                    nc.gpsimd.tensor_tensor(half2[:, :, :], half1[:, :, 0:2 * C], half1[:, :, 2 * C:], ALU.add)\
                        .then_inc(pool_add, 1)
                    pool.wait_ge(pool_add, m.at(14, 2 * n + 2))
                    nc.gpsimd.tensor_tensor(ffn[:, 4 * n:4 * n + 4, :], half2[:, :, 0:C], half2[:, :, C:], ALU.add)\
                        .then_inc(ffn_made, 1)

            walk(pool, step)

        @block.vector
        def _(dve):
            own = [0]
            chain = sem("chain")

            def link(ins):
                own[0] += 1
                ins.then_inc(chain, 1)
                dve.wait_ge(chain, own[0])

            v = nc.vector
            v.memset(minus_one, -1.0)
            v.memset(den_eps, DEN_EPS * SHIFT)
            v.memset(nat[:, :, :], 1.0)
            v.memset(dmat[:, :, :, :], 0.0)
            for ln in range(2):
                link(v.memset(xn[ln][:, :, C - 1:C], 1.0))
            with dve.Fori(0, 4) as t:
                for k in range(2):
                    for b in range(4):
                        img = t * 8 + (4 * k + b)
                        dve.wait_ge(stage_turned, img + 1)
                        for h in range(2):
                            last = v.bn_stats(stats[:, bass.ds(img, 1), 6 * h:6 * h + 6].rearrange("p a k -> p (a k)"),
                                              ps[:, 2 * b + h, 0:HALF[h] * PT])
                        last.then_inc(stage_read, 1)
            dve.wait_ge(stage_read, B)
            dve.wait_ge(consts_in, 16 * 25)
            for b in range(B):
                last = v.bn_aggr(mv[:, b, :], stats[:, b, :])
            link(last)
            v.tensor_copy(bw[:, 0, :], mv[:, :, 0]).then_inc(dve_pre, 1)
            dve.wait_ge(pe_pre, 1)
            link(v.tensor_copy(bw[:, 1, :], ps[:, 0, 0:B]))
            link(v.tensor_tensor(bw[:, 5, :], mv[:, :, 0], bw[:, 1, :], ALU.subtract))
            link(v.tensor_tensor(bw[:, 6, :], bw[:, 5, :], bw[:, 5, :], ALU.mult))
            v.tensor_tensor(bw[:, 2, :], mv[:, :, 1], bw[:, 6, :], ALU.add).then_inc(dve_pre, 1)
            link(v.tensor_tensor(wva_s, wva_s, wvb_s, ALU.subtract))
            for h in range(HEADS):
                if h >= 2:
                    dve.wait_ge(pe_pre, 2 + h - 1)
                o = 128 * (h % 2)
                v.tensor_copy(xres[0:32, o:o + 128].rearrange("p (k a) -> p k a", k=4),
                              wva_s[:, C * h:C * h + C].unsqueeze(1).to_broadcast([32, 4, C])).then_inc(dve_pre, 1)
            dve.wait_ge(pe_pre, 2 + HEADS)
            v.tensor_scalar(minus_one, minus_one, 1.0, None, ALU.mult).then_inc(dve_pre, 1)
            link(v.tensor_scalar(bw[:, 3, :], ps[:, 1, 0:B], GN_EPS, None, ALU.add))
            link(v.tensor_copy(bw[:, 7, :], ps[:, 1, 0:B]))
            v.tensor_copy(small[:, 12:13], small[:, 0:1]).then_inc(dve_pre, 1)
            dve.wait_ge(pool_pre, 2)
            link(v.tensor_tensor(bw[:, 5, :], bw[:, 7, :], bw[:, 4, :], ALU.mult))
            link(v.tensor_tensor(bw[:, 6, :], bw[:, 5, :], bw[:, 4, :], ALU.mult))
            link(v.tensor_reduce(bn_gain, bw[:, 6, :], AX_X, ALU.add))
            v.tensor_scalar(bn_half, bn_gain, 1.0 / B, BN_EPS, ALU.mult, ALU.add).then_inc(dve_pre, 1)
            dve.wait_ge(pool_pre, 3)
            link(v.tensor_tensor(bn_gain, bn_inv, gamma_c, ALU.mult))
            link(v.tensor_scalar(bin_a[:, :], bw[:, 4, :], bn_gain, None, ALU.mult))
            link(v.tensor_tensor(bw[:, 5, :], bin_a[:, :], bw[:, 1, :], ALU.mult))
            link(v.tensor_scalar(bin_thr[:, :], bw[:, 5, :], beta_c, None, ALU.subtract))
            rows, rows2, tmp = views["rows"], views["rows2"], views["tmp"]
            link(v.tensor_scalar(rows2, rows, -1.0, None, ALU.mult))
            link(v.tensor_tensor(rows2, rows2, rows, ALU.max))
            link(v.tensor_reduce(conv_scale, rows2, AX_X, ALU.add))
            link(v.tensor_scalar(conv_scale, conv_scale, 1.0 / (9 * C), None, ALU.mult))
            link(v.tensor_scalar(rows2, rows, 0.0, 2.0, ALU.is_ge, ALU.mult))
            link(v.tensor_scalar(rows2, rows2, -1.0, None, ALU.add))
            link(v.tensor_reduce(conv_sum, rows2, AX_X, ALU.add))
            link(v.tensor_tensor(conv_bias, conv_scale, conv_sum, ALU.mult))
            link(v.tensor_scalar(conv_bias, conv_bias, -1.0, None, ALU.mult))
            link(v.tensor_scalar(conv_scale2, conv_scale, 2.0, None, ALU.mult))
            link(v.tensor_scalar(tmp, views["taps"], 0.0, 2.0, ALU.is_ge, ALU.mult))
            link(v.tensor_scalar(tmp, tmp, -1.0, None, ALU.add))
            link(v.tensor_tensor(conv_w[:, :, :].rearrange("p a b -> p (a b)"), tmp, views["valid"], ALU.mult))
            for dst, a, b, w in ((wq16, views["wqa"], wqb_s, DH), (wk16, views["wka"], wkb_s, DH),
                                 (we16, views["wea"], web_s, 264)):
                link(v.tensor_tensor(a, a, b, ALU.subtract))
                link(v.tensor_copy(dst[:, 0:w], a))
                link(v.tensor_tensor(dst[64:128, 0:w], a[64:128], dst[64:128, 0:w], ALU.subtract))
            v.tensor_copy(eye16[:, :], eye_center[:, 0:128]).then_inc(eye16_made, 1)
            link(v.tensor_copy(sel16[:, 0:1024], sel_s[0]))
            link(v.tensor_copy(sel16[:, 1024:2048], qflat[:, at:at + 1024]))
            dve.wait_ge(act_pre, 1)
            v.tensor_copy(small[:, 12:13], small[:, 0:1]).then_inc(dve_pre, 1)

            def step(kind, m, n, done, it):
                if kind in RING:
                    s, no = ring_no(done, it)
                    o = ring(s)
                if kind in MISC:
                    s, no = misc_no(done, it)
                    o = misc(s)
                if kind == "XT":
                    dve.wait_ge(misc_full, no + 1)
                    if n == 0:
                        wait(dve, shift_in, m.at(64))
                    w = HALF[n]
                    dst = nat[:, 1:1 + PR, 1:1 + PR].rearrange("p (y j) x -> p j y x", j=TILES)[:, 4 * n:4 * n + w]
                    i = bass.ds(m.at(1), 1) if m.t is not None else slice(m.c, m.c + 1)
                    for y in range(YL):
                        last = v.tensor_scalar(dst[:, :, y, :],
                                               o[:, 0:w * PT].rearrange("p (j y x) -> p j y x", j=w, y=YL)[:, :, y, :],
                                               bin_a[:, i], bin_thr[:, i], ALU.mult, ALU.is_ge)
                    last.then_inc(binarized, 1)
                elif kind == "CV":
                    dve.wait_ge(misc_full, no + 1)
                    dve.wait_ge(xres_made, m.at(2, n + 1))
                    if n == 0:
                        wait(dve, t1b_made, m.at(1, -1))
                    a, b = COL[n]
                    v.scalar_tensor_tensor(t1[:, m.par, a:b], o[:, 0:b - a], conv_scale2, xres[:, a:b], ALU.mult,
                                           ALU.add).then_inc(t1_made, 1)
                elif kind in ("SM1", "SM2"):
                    ln = kind == "SM2"
                    if ln:
                        dve.wait_ge(t2_made, m.at(4, 4))
                    else:
                        dve.wait_ge(xc_made[0], m.at(2, 2))
                    v.tensor_reduce(ssum[ln][:, :], sq[ln][:, :, :], AX_X, ALU.add).then_inc(ssum_made[ln], 1)
                    dve.wait_ge(ssum_made[ln], m.at(1, 1))
                    wait(dve, rstd_made[ln], m.at(1))
                    v.tensor_scalar(varr[ln][:, :], ssum[ln][:, :], 1.0 / C, LN_EPS, ALU.mult, ALU.add)\
                        .then_inc(var_made[ln], 1)
                elif kind == "K":
                    dve.wait_ge(kexp_made, m.at(14, n + 1))
                    wait(dve, ktx_done, m.at(14, n - 1))
                    v.scalar_tensor_tensor(kbuf[:, n % 2, :].rearrange("p (a b) -> p a b", a=2), o[0:PT, :, :], 1.0,
                                           ebuf[0:PT, n % 2, :].rearrange("p (a b) -> p a b", a=2), ALU.max, ALU.min)\
                        .then_inc(k_made, 1)
                elif kind == "Q":
                    j, k0 = n // 2, 2 * (n % 2)
                    dve.wait_ge(qexp_made, m.at(14, n + 1))
                    v.scalar_tensor_tensor(qbuf[:, k0:k0 + 2, j, :], o[:, :, 0:G * PT], 1.0,
                                           ebuf[:, n % 2, 0:2 * G * PT].rearrange("p (a b) -> p a b", a=2), ALU.max,
                                           ALU.min).then_inc(q_made, 1)
                elif kind == "DN" and n in (3, 6):
                    h = n // 4
                    a, b = COL[h]
                    dve.wait_ge(nd_full, nd_no(done, it) + 1)
                    wait(dve, den_made, m.at(2))
                    v.tensor_tensor(dcs[:, a:b], nd_bank[:, 0:b - a], tabd[:, a:b], ALU.mult).then_inc(nd_read, 1)
                elif kind == "RC":
                    a, b = COL[n]
                    dve.wait_ge(den_made, m.at(2, n + 1))
                    v.reciprocal(den[:, a:b], den[:, a:b]).then_inc(recip_made, 1)
                    dve.wait_ge(recip_made, m.at(2, n + 1))
                    v.tensor_copy(rs[:, a:b], den[:, a:b]).then_inc(rhigh_made, 1)
                    dve.wait_ge(rhigh_made, m.at(2, n + 1))
                    v.tensor_tensor(rs[64:128, a:b], den[64:128, a:b], rs[64:128, a:b], ALU.subtract)\
                        .then_inc(r_made, 1)
                elif kind == "R":
                    j, k0 = n // 2, 2 * (n % 2)
                    dve.wait_ge(ring_full, no + 1)
                    v.tensor_tensor(qbuf[:, k0:k0 + 2, j, :], o[:, :, 0:G * PT], qbuf[:, k0:k0 + 2, j, :], ALU.mult)\
                        .then_inc(qr_made, 1)
                elif kind == "NM":
                    w = min(2, TILES - 2 * n)
                    dve.wait_ge(nd_full, nd_no(done, it) + 1)
                    if n == 0:
                        wait(dve, t2_made, m.at(4))
                    v.tensor_tensor(pbuf[:, 2 * n:2 * n + w, :, :].rearrange("p j a t -> p (j a t)"),
                                    nd_bank[:, 0:2 * PT * w],
                                    tabn[:, 2 * n:2 * n + w, :].rearrange("p j t -> p (j t)"), ALU.mult)\
                        .then_inc(nd_read, 1)
                elif kind == "LG":
                    dve.wait_ge(ring_full, no + 1)
                    shape = [PT, SLOTS, EXPERTS]

                    def grid(a):
                        return a.rearrange("p (s e) -> p s e", e=EXPERTS)

                    def spread(a):
                        return a.unsqueeze(2).to_broadcast(shape)

                    logits, hot1, hot2, rest = (route[:, k, :] for k in range(4))
                    top1, top2, diff, ratio, w1, w2 = (rmax[:, k, :] for k in range(6))
                    k = [0]

                    def tick(ins):
                        k[0] += 1
                        ins.then_inc(route_step, 1)
                        dve.wait_ge(route_step, m.at(18, k[0]))

                    tick(v.tensor_copy(logits, o[0:PT, 0, 0:SLOTS * EXPERTS]))
                    for top, src, hot, w in ((top1, logits, hot1, w1), (top2, rest, hot2, w2)):
                        if src is rest:
                            tick(v.scalar_tensor_tensor(rest, hot1, -3.0e38, logits, ALU.mult, ALU.add))
                        tick(v.tensor_reduce(top, grid(src), AX_X, ALU.max))
                        tick(v.tensor_tensor(grid(hot), grid(src), spread(top), ALU.is_equal))
                        tick(v.tensor_tensor(hot, hot, first[:, :], ALU.mult))
                        tick(v.tensor_reduce(w, grid(hot), AX_X, ALU.max))
                        tick(v.tensor_tensor(grid(hot), grid(hot), spread(w), ALU.is_equal))
                    tick(v.tensor_tensor(diff, top2, top1, ALU.subtract))
                    dve.wait_ge(ratio_made, m.at(1, 1))
                    tick(v.tensor_scalar(w1, ratio, 1.0, None, ALU.add))
                    tick(v.reciprocal(w2, w1))
                    tick(v.tensor_tensor(w1, ratio, w2, ALU.mult))
                    tick(v.tensor_tensor(grid(hot1), grid(hot1), spread(w2), ALU.mult))
                    tick(v.tensor_tensor(grid(hot2), grid(hot2), spread(w1), ALU.mult))
                    assert k[0] == 18
                    v.tensor_tensor(gate[:, :], hot1, hot2, ALU.add).then_inc(gate_made, 1)
                elif kind == "F":
                    dve.wait_ge(ring_full, no + 1)
                    if n == 0:
                        dve.wait_ge(gate_made, m.at(1, 1))
                    wait(dve, ffn_made, m.at(7, max(n - 1, 0)))
                    w = 4 * EXPERTS
                    v.tensor_tensor(prod[:, n % 2, :, :].rearrange("p s (e c) -> p (s e) c", c=C),
                                    o[0:PT, :, :].rearrange("p k (s c) -> p (k s) c", c=C),
                                    gate[:, w * n:w * n + w].unsqueeze(2).to_broadcast([PT, w, C]), ALU.mult)\
                        .then_inc(prod_made, 1)
                elif kind == "OUT":
                    dve.wait_ge(ffn_made, m.at(7, 7))
                    f = ffn[:, :, :].rearrange("p s c -> p (s c)")
                    v.tensor_tensor(f, f, t2[:, :], ALU.add).then_inc(out_made, 1)

            walk(dve, step)


def kernel(**inputs):
    import numpy as _np
    import concourse.bacc as _bacc
    from concourse import mybir as _mybir
    from concourse.bass_utils import run_bass_kernel_spmd as _run

    get = {k: _np.ascontiguousarray(v) for k, v in inputs.items()}
    f = _np.float32

    def column(a):
        return _np.ascontiguousarray(_np.tile(a, G)[:, None])

    def folded(w, b, const, copies):
        n = w.shape[1]
        a = _np.concatenate([w[0:C - 1], b[None, :]], 0)
        r = _np.concatenate([_np.tile(w[C - 1:C], (C - 1, 1)), _np.full((1, n), const, f)], 0)
        return _np.stack([_np.tile(a, (copies, 1)), _np.tile(r, (copies, 1))])

    conv = get["L0_conv_W"]
    taps = _np.zeros((G, C, 2, 2, G, C), f)
    for kh, kw, gi, i, j, go in _taps():
        taps[gi, :, i, j, go, :] = conv[kh, kw]
    rows = _np.tile(conv.reshape(9 * C, C).T, (G, 1))
    wq = folded(get["L1_attn_wq_w"].T, get["L1_attn_wq_b"], -1.0, 4)
    wk = folded(get["L1_attn_wk_w"].T, get["L1_attn_wk_b"], -1.0, 4)
    wv = folded(get["L1_attn_wv_w"].T, get["L1_attn_wv_b"], 0.0, 1)
    wv = wv.reshape(2, C, HEADS, C).transpose(0, 3, 2, 1).reshape(2, C, DH)
    wd = get["L1_attn_dense_w"].reshape(C, HEADS, C).transpose(2, 1, 0).reshape(C, DH)
    expert = get["L1_ffn_expert_w"].transpose(1, 0, 2).reshape(C, EXPERTS * C)
    we = folded(_np.concatenate([expert, get["L1_ffn_router_w"]], 1),
                _np.concatenate([get["L1_ffn_expert_b"].reshape(-1), get["L1_ffn_router_b"]]), 0.0, 4)
    c = consts()
    arrays = dict(x=get["x"], gamma=column(get["L0_conv_gamma"]), beta=column(get["L0_conv_beta"]),
                  conv_taps=taps.reshape(128, 512), conv_rows=rows, wq=wq, wk=wk, wv=wv, wd=wd,
                  wd_b=column(get["L1_attn_dense_b"]), we=we, eyec=c["eyec"], mean4=c["mean4"], pair=c["pair"],
                  dsum=c["dsum"], sel=c["sel"], p2c=c["p2"], tabdc=c["tabd"], tabnc=c["tabn"], tabkc=c["tabk"],
                  firstc=c["first"], validc=c["valid"])
    nc = _bacc.Bacc("TRN2", target_bir_lowering=False, num_devices=1)
    arrays = {k: _np.ascontiguousarray(a) for k, a in arrays.items()}
    args = {k: nc.dram_tensor(f"in_{k}", a.shape, _mybir.dt.from_np(a.dtype), kind="ExternalInput").ap()
            for k, a in arrays.items()}
    out = nc.dram_tensor("out_0", (B, HW, HW, C), F32, kind="ExternalOutput").ap()
    build(nc, out=out, **args)
    r = _run(nc, [{f"in_{k}": a for k, a in arrays.items()}], core_ids=[0])
    return r.results[0]["out_0"]
```

```python
from contextlib import ExitStack

import concourse.bass as bass
import numpy as np
from concourse import mybir

F32 = mybir.dt.float32
F16 = mybir.dt.float16
BF16 = mybir.dt.bfloat16
ALU = mybir.AluOpType
ACT = mybir.ActivationFunctionType
AX_X = mybir.AxisListType.X

B, HW, C = 32, 56, 32
HEADS, EXPERTS = 16, 8
PR = HW // 2
G = 4
TILES = 7
YL = PR // TILES
PT = YL * PR
SLOTS = TILES * G
PATCHES = TILES * PT
TOKENS = HW * HW
DH = HEADS * C
CH = DH // 128
HPC = HEADS // CH
PITCH = PR + 2
HALF = (4, 3)
COL = [(0, 4 * PT), (4 * PT, 7 * PT)]
HW4 = G * PT
LN_EPS, GN_EPS, BN_EPS = 1e-5, 1e-5, 1e-3
DEN_EPS = 1e-5
SHIFT = 2.0 ** -22


def consts():
    eye = np.eye(128, dtype=np.float32)
    i32 = np.eye(32, dtype=np.float32)
    center = np.kron(np.eye(4), i32 - 1.0 / 32).astype(np.float32)
    mean4 = np.kron(np.ones((4, 4)), i32 / 4).astype(np.float32)
    pair = np.concatenate([np.kron(np.eye(2), np.kron(np.ones((2, 1)), m))
                           for m in (i32, i32 - 1.0 / 32)], 1).astype(np.float32)
    dsum = np.kron(np.eye(4), np.kron(np.ones((2, 1)), np.eye(16)))
    dsum = np.concatenate([dsum, dsum], 1).astype(np.float32)
    sel = np.zeros((2, 4, HEADS, CH, 4, HPC, 32), np.float32)
    for j in range(4):
        for h in range(HEADS):
            sel[:, j, h, h // HPC, j, h % HPC, :] = 1.0
    p2 = np.zeros((2, 2, 32, CH, 2, HPC, 33), np.float32)
    for cs in range(2):
        p2[:, cs, 31, :, cs, :, 32] = SHIFT
    tile, g, yl, px = np.meshgrid(np.arange(TILES), np.arange(G), np.arange(YL), np.arange(PR), indexing="ij")
    row, col = 2 * (TILES * yl + tile) + g // 2, 2 * px + g % 2
    s = (row * HW + col).reshape(TILES, G, PT)
    pos = np.float32(1.57) * np.arange(TOKENS, dtype=np.float32) / np.float32(TOKENS)
    cs = np.stack([np.cos(pos), np.sin(pos)]).astype(np.float32)[:, s]
    tabd = np.zeros((4, 2, HEADS, 2, HW4), np.float32)
    for j in range(TILES):
        tabd[j % 4, :, :, j // 4] = cs[:, j].reshape(2, 1, HW4)
    v = cs.reshape(2, TILES, 2, 2, PT)
    tabn = np.repeat(v.transpose(3, 0, 1, 2, 4)[:, :, None], 32, 2).reshape(128, 2 * PATCHES)
    tabk = cs.transpose(3, 0, 1, 2).reshape(PT, 2 * SLOTS)
    first = np.tile(np.arange(EXPERTS, 0, -1, dtype=np.float32), (PT, SLOTS))
    valid = np.zeros((G, 32, 2, 2, G, 32), np.float32)
    for (di, dj, gi, i, j, go) in _taps():
        valid[gi, :, i, j, go, :] = 1.0
    return dict(eyec=np.concatenate([eye, center], 1), mean4=mean4, pair=pair, dsum=dsum,
                sel=sel.reshape(128, -1), p2=p2.reshape(128, -1), tabd=tabd.reshape(128, -1), tabn=tabn, tabk=tabk,
                first=first, valid=valid.reshape(128, -1))


def _taps():
    for gi in range(G):
        for go in range(G):
            for i in range(2):
                for j in range(2):
                    kh = 2 * i + 1 - gi // 2 - go // 2
                    kw = 2 * j + 1 - gi % 2 - go % 2
                    if 0 <= kh <= 2 and 0 <= kw <= 2:
                        yield kh, kw, gi, i, j, go


class Img:

    def __init__(self, t, c):
        self.t, self.c = t, c

    def at(self, per, off=0):
        return self.c * per + off if self.t is None else self.t * (2 * per) + (self.c * per + off)

    @property
    def par(self):
        return self.c % 2


PERIOD = 14
RING_SLOTS = 3
RING = ("K", "R", "Q", "G", "LG", "F", "XC", "ZT", "ZU")
MISC = ("XT", "CV", "DN", "SU", "NM", "T2")


def schedule():
    s = []

    def add(kind, times):
        s.extend((t, kind, n) for n, t in enumerate(times))

    add("XT", [-17.16, -16.39])
    add("CV", [-14.36, -14.09])
    add("XC", [-13.41])
    add("SM1", [-13.21])
    add("PN1", [-11.36])
    add("XH1", [-11.15])
    add("PL1", [-10.38])
    add("CS", [-10.12, -2.25])
    add("ZT", [-9.65, -8.79])
    add("K", [-6.94, -5.27, -4.45, -3.51, -2.73, -2.19, -0.05, 0.47, 0.99, 2.24, 3.44, 4.57, 4.84, 6.61])
    add("KX", [-5.50, -4.10, -3.47, -2.11, -0.84, -0.07, 0.79, 2.25, 3.41, 3.57, 4.65, 6.50, 6.90, 7.60])
    add("KT", [8.00])
    add("G", [8.20, 8.42])
    add("Q", [-0.15, 0.32, 2.92, 3.70, 4.55, 4.67, 6.15, 6.79, 7.81, 8.54, 10.06, 12.92, 13.21, 13.62])
    add("DN", [8.64, 8.73, 8.79, 9.08, 14.00, 14.45, 14.55, 15.14])
    add("SU", [9.54, 15.67])
    add("RC", [9.73, 16.04])
    add("R", [10.86, 11.38, 13.04, 13.84, 14.66, 15.66, 15.67, 17.12, 19.17, 19.65, 21.15, 22.37, 22.45, 23.30])
    add("NM", [13.28, 15.79, 18.15, 18.71, 20.65, 23.77, 25.28])
    add("TB", [14.13])
    add("T2", [16.62, 19.95, 24.49, 26.03])
    add("SM2", [26.80])
    add("PN2", [27.48])
    add("XH2", [28.73])
    add("PL2", [26.72])
    add("ZU", [29.26, 29.86])
    add("LG", [30.41])
    add("RT", [30.60, 30.76, 31.24, 31.90, 32.13, 32.89, 33.65])
    add("F", [34.05, 35.00, 35.78, 36.33, 36.51, 37.47, 37.54])
    add("OUT", [42.50])
    return sorted(s)


SCHEDULE = schedule()
SHIFTS = {
    "tensor": {},
    "vector": {"CV": -0.25, "DN": -0.29, "K": 0.01, "LG": 0.06, "NM": -0.07, "OUT": 0.52, "Q": 0.02,
               "RC": -0.01, "RT": 0.08, "SM1": -0.05, "SM2": -0.26, "T2": 0.08, "XT": -0.39},
    "scalar": {"G": -0.14, "K": -0.11, "KT": -0.4, "Q": -0.11, "RT": 0.44, "SU": -0.42, "T2": -0.04,
               "TB": -0.69, "XC": 0.24, "XH1": -1.29, "XH2": -0.61, "XT": -0.28, "ZT": -0.38, "ZU": -0.33},
    "gpsimd": {"CS": 0.64, "F": -2.19, "PL1": 0.22, "PL2": 0.77, "PN1": -0.22, "PN2": -0.05},
    "sync": {"CV": -0.66, "OUT": 2.93, "XT": -8.67},
}
LOOP_FIRST, LOOP_LAST = 3, B - 4


def iteration(engine, i):
    shift = SHIFTS[engine]
    steps = sorted((t + shift.get(kind, 0), t, kind, n) for t, kind, n in SCHEDULE)
    out = []
    for t, t0, kind, n in steps:
        d = int(t // PERIOD)
        out.append((t - PERIOD * d, t0, kind, i - d, n))
    return [(kind, m, n) for _, _, kind, m, n in sorted(out) if 0 <= m < B]


ITERATIONS = range(-3, B + 3)


def rounds(kinds, slots):
    order = []
    for i in ITERATIONS:
        for kind, m, n in iteration("tensor", i):
            key = (kind, m, n // 4 if kind == "DN" else n)
            if kind in kinds and (not order or order[-1] != key):
                order.append(key)
    assert len(order) == len(set(order))
    return {key: (k % slots, k, order[k - slots] if k >= slots else None) for k, key in enumerate(order)}


def walk(eng, name, step):
    tables = [rounds(RING, RING_SLOTS), rounds(MISC, 1)]

    def lookup(kind, m, n, t):
        if kind not in RING and kind not in MISC:
            return None
        table = tables[kind in MISC]
        n = n // 4 if kind == "DN" else n
        slot, no, before = table[kind, m, n]
        if t is not None:
            (_, no2, before2), last = table[kind, m + 2, n], LOOP_LAST - LOOP_FIRST - 1
            slot_z, no_z, before_z = table[kind, m + last, n]
            assert no_z == no + (no2 - no) * (last // 2) and slot_z == slot
            assert before_z == (before[0], before[1] + last, before[2])
            no = t * (no2 - no) + no
        if before is not None:
            before = (before[0], Img(t, before[1]), before[2])
        return slot, no, before

    def run(i, t=None):
        for kind, m, n in iteration(name, i):
            step(kind, Img(t, m), n, lookup(kind, m, n, t))

    for i in ITERATIONS:
        if i < LOOP_FIRST:
            run(i)
    with eng.Fori(0, (LOOP_LAST + 1 - LOOP_FIRST) // 2) as t:
        run(LOOP_FIRST, t)
        run(LOOP_FIRST + 1, t)
    for i in ITERATIONS:
        if i > LOOP_LAST:
            run(i)


def build(nc, x, gamma, beta, conv_taps, conv_rows, wq, wk, wv, wd, wd_b, we, eyec, mean4, pair, dsum, sel,
          p2c, tabdc, tabnc, tabkc, firstc, validc, out):
    ctx = ExitStack()
    with ctx:
        def sb(name, shape, dt=F32):
            return ctx.enter_context(nc.sbuf_tensor(name, shape, dt))

        def sem(name):
            return ctx.enter_context(nc.semaphore(name))

        eye_center = sb("eye_center", [128, 256])
        mean4_sb = sb("mean4_sb", [128, 128])
        pair_sb = sb("pair_sb", [128, 128])
        dsum_sb = sb("dsum_sb", [128, 128])
        eye16 = sb("eye16", [128, 128], F16)
        sel16 = sb("sel16", [128, CH * G * 128], F16)
        p2 = sb("p2", [128, CH, 2, HPC, 33])
        tabd = sb("tabd", [128, 2, HW4])
        tabn = sb("tabn", [128, TILES, 2 * PT])
        tabk = sb("tabk", [PT, 2, SLOTS])
        first = sb("first", [PT, SLOTS * EXPERTS])
        conv_w = sb("conv_w", [128, 4, 128], BF16)
        wq16 = sb("wq16", [128, DH], F16)
        wk16 = sb("wk16", [128, DH], F16)
        we16 = sb("we16", [128, EXPERTS * C + EXPERTS], F16)
        small = sb("small", [128, 16])
        gamma_c, beta_c, dense_b = (small[:, k:k + 1] for k in range(3))
        conv_scale, conv_sum, conv_bias, conv_scale2 = (small[:, k:k + 1] for k in range(3, 7))
        minus_one, den_eps, bn_inv, bn_half = (small[:, k:k + 1] for k in range(7, 11))
        bn_gain = small[:, 11:12]
        bin_a = sb("bin_a", [128, B])
        bin_thr = sb("bin_thr", [128, B])
        power = sb("power", [128, B])
        xt = sb("xt", [PT, TILES * G * C])
        nat = sb("nat", [128, PITCH, PITCH], BF16)
        shifted = sb("shifted", [128, PITCH, PITCH], BF16)
        xres = sb("xres", [128, PATCHES])
        t1 = sb("t1", [128, 2, PATCHES])
        t1b = sb("t1b", [128, PATCHES])
        xc = [sb(f"xc{k}", [PT, SLOTS, C]) for k in (1, 2)]
        sq1 = sb("sq1", [PT, SLOTS, C])
        sq2 = sb("sq2", [PT, 2, 2 * G, C])
        xn = [sb(f"xn{k}", [PT, SLOTS, C]) for k in (1, 2)]
        parts = [sb(f"parts{k}", [PT, SLOTS, 2 * C], F16) for k in (1, 2)]
        ssum = [sb(f"ssum{k}", [PT, SLOTS]) for k in (1, 2)]
        varr = [sb(f"varr{k}", [PT, SLOTS]) for k in (1, 2)]
        rstd = [sb(f"rstd{k}", [PT, SLOTS]) for k in (1, 2)]
        xcs = sb("xcs", [PT, SLOTS, 2, C])
        z1 = sb("z1", [128, 2, SLOTS * PT], F16)
        z2 = sb("z2", [128, SLOTS * PT], F16)
        ebuf = sb("ebuf", [128, 2, 1024])
        kbuf = sb("kbuf", [PT, 2, 1024])
        ktsb = sb("ktsb", [128, DH])
        gmat = sb("gmat", [128, 2, CH, 2, C])
        dmat = sb("dmat", [128, 2, CH, 2, HEADS])
        qbuf = sb("qbuf", [128, CH, TILES, G * PT])
        dcs = sb("dcs", [128, HW4])
        den = sb("den", [128, HW4])
        rs = sb("rs", [128, 2, HW4], F16)
        pbuf = sb("pbuf", [128, 4, 2, PT])
        t2 = sb("t2", [PT, 2, TILES * G * C])
        route = sb("route", [PT, 4, SLOTS * EXPERTS])
        rmax = sb("rmax", [PT, 6, SLOTS])
        gate = sb("gate", [PT, SLOTS * EXPERTS])
        prod = sb("prod", [PT, 2, 4, EXPERTS * C])
        ffn = sb("ffn", [PT, SLOTS, C])
        qflat = qbuf[:, :, :, :].rearrange("p a b c -> p (a b c)")
        stage = [qflat[0:PT, k * 3584:(k + 1) * 3584].rearrange("p (b f) -> p b f", b=4) for k in range(2)]
        at, views = 2 * 3584, {}
        for name, width in (("taps", 512), ("valid", 512), ("rows", 288), ("wqa", DH), ("wka", DH),
                            ("wea", 264), ("tmp", 512), ("sel", CH * 4 * 128)):
            views[name] = qflat[:, at:at + width]
            at += width
        assert at <= CH * TILES * G * PT
        wqb_s, wkb_s, web_s = ebuf[:, 0, 0:DH], ebuf[:, 0, DH:2 * DH], ebuf[:, 1, 0:264]
        wva_s, wvb_s = t1[0:32, 0, 0:DH], t1[0:32, 1, 0:DH]
        wd_s = t1b[0:32, 0:DH]
        wvr = xres[0:32, 0:128]
        views["rows2"] = xres[:, 256:256 + 9 * C]
        stats = dcs[:, 0:B * 12].rearrange("p (b k) -> p b k", b=B)
        mv = den[:, 0:B * 2].rearrange("p (b k) -> p b k", b=B)
        bw = den[:, 64:64 + 8 * B].rearrange("p (k b) -> p k b", k=8)

        ps = ctx.enter_context(nc.psum_tensor("ps", [128, 8, 512], F32))

        def ring(s):
            return ps[:, 2 * s:2 * s + 2, :]

        def misc():
            return ps[:, 2 * RING_SLOTS, :]

        kt_bank = ps[:, 2 * RING_SLOTS + 1, :]

        consts_in = sem("consts_in")
        eye_in = sem("eye_in")
        stage_in = [sem(f"stage_in{k}") for k in range(2)]
        stage_turned = sem("stage_turned")
        stage_read = sem("stage_read")
        pe_pre = sem("pe_pre")
        eye16_made = sem("eye16_made")
        dve_pre = sem("dve_pre")
        pool_pre = sem("pool_pre")
        act_pre = sem("act_pre")
        x_in = sem("x_in")
        shift_in = sem("shift_in")
        out_stored = sem("out_stored")
        ring_full = sem("ring_full")
        misc_full = sem("misc_full")
        dcs_made = sem("dcs_made")
        numer_made = sem("numer_made")
        binarized = sem("binarized")
        xres_made = sem("xres_made")
        t1_made = sem("t1_made")
        xc_made = [sem(f"xc_made{k}") for k in (1, 2)]
        piece_summed = sem("piece_summed")
        ssum_made = [sem(f"ssum_made{k}") for k in (1, 2)]
        var_made = [sem(f"var_made{k}") for k in (1, 2)]
        rstd_made = [sem(f"rstd_made{k}") for k in (1, 2)]
        xn_made = [sem(f"xn_made{k}") for k in (1, 2)]
        high_made = [sem(f"high_made{k}") for k in (1, 2)]
        parts_made = [sem(f"parts_made{k}") for k in (1, 2)]
        z_made = [sem(f"z_made{k}") for k in (1, 2)]
        xcs_made = sem("xcs_made")
        kexp_made = sem("kexp_made")
        qexp_made = sem("qexp_made")
        k_made = sem("k_made")
        q_made = sem("q_made")
        ktx_done = sem("ktx_done")
        kt_copied = sem("kt_copied")
        g_made = sem("g_made")
        den_made = sem("den_made")
        recip_made = sem("recip_made")
        rhigh_made = sem("rhigh_made")
        r_made = sem("r_made")
        qr_made = sem("qr_made")
        t1b_made = sem("t1b_made")
        t2_made = sem("t2_made")
        route_step = sem("route_step")
        ratio_made = sem("ratio_made")
        gate_made = sem("gate_made")
        prod_made = sem("prod_made")
        pool_add = sem("pool_add")
        ffn_made = sem("ffn_made")
        out_made = sem("out_made")

        def wait(eng, s, v):
            if not isinstance(v, int) or v > 0:
                eng.wait_ge(s, v)

        READ = {"K": (k_made, 14), "R": (qr_made, 14), "Q": (q_made, 14), "G": (g_made, 2), "LG": (route_step, 18),
                "F": (prod_made, 7), "XC": (xc_made[0], 1), "ZT": (z_made[0], 2), "ZU": (z_made[1], 2),
                "XT": (xres_made, 2), "CV": (t1_made, 2), "DN": (dcs_made, 2), "SU": (den_made, 2),
                "NM": (numer_made, 7), "T2": (t2_made, 4)}

        block = ctx.enter_context(nc.Block())

        @block.sync
        def _(sp):
            sp.dma_start(eye_center[:, :], eyec).then_inc(eye_in, 16)
            for dst, src in ((mean4_sb[:, :], mean4), (views["rows"], conv_rows),
                             (small[:, 0:1], gamma), (small[:, 1:2], beta), (small[:, 2:3], wd_b)):
                sp.dma_start(dst, src).then_inc(consts_in, 16)
            x4 = x.rearrange("(q b) h w c -> q b (h w c)", b=4).rearrange("q b (p f) -> q p b f", p=PT)

            def stage_load(q, k, turned):
                wait(sp, stage_turned, turned)
                sp.dma_start(stage[k], q).then_inc(stage_in[k], 16)

            for k in range(2):
                stage_load(x4[k], k, 0)
            for dst, src in ((pair_sb[:, :], pair), (dsum_sb[:, :], dsum), (views["taps"], conv_taps),
                             (views["valid"], validc), (views["wqa"], wq[0]), (wqb_s, wq[1]), (views["wka"], wk[0]),
                             (wkb_s, wk[1]), (views["wea"], we[0]), (web_s, we[1]), (wva_s, wv[0]), (wvb_s, wv[1]),
                             (wd_s, wd), (p2[:, :, :, :, :].rearrange("p a b c d -> p (a b c d)"), p2c),
                             (tabd[:, :, :].rearrange("p a b -> p (a b)"), tabdc), (tabk[:, :, :].rearrange("p a b -> p (a b)"), tabkc),
                             (first[:, :], firstc), (views["sel"], sel),
                             (tabn[:, :, :].rearrange("p a b -> p (a b)"), tabnc)):
                sp.dma_start(dst, src).then_inc(consts_in, 16)
            with sp.Fori(1, 4) as t:
                for k in range(2):
                    wait(sp, stage_turned, t * 8 + (4 * k - 4))
                    sp.dma_start(stage[k], x4[bass.ds(t * 2 + k, 1)].rearrange("q p b f -> (q p) b f"))\
                        .then_inc(stage_in[k], 16)

            xt_v = xt[:, :].rearrange("p (j d e) -> p j d e", j=TILES, d=2)

            def rows_of(a, m, yl):
                img = a[m.at(1):m.at(1) + 1] if m.t is None else a[bass.ds(m.at(1), 1)]
                return img.rearrange("b (q j d) (z e) c -> (b q) z (j d) (e c)", j=TILES, d=2, e=2)[yl]

            def load(m):
                for yl in range(YL):
                    sp.dma_start(xt_v[PR * yl:PR * yl + PR].rearrange("p j d e -> p (j d) e"), rows_of(x, m, yl))\
                        .then_inc(x_in, 16)

            def step(kind, m, n, rd):
                if kind == "XT" and n == 0:
                    wait(sp, xres_made, m.at(2))
                    load(m)
                if kind == "CV" and n == 0:
                    sp.wait_ge(binarized, m.at(2, 2))
                    wait(sp, t1_made, m.at(2))
                    for g in range(G):
                        dy, dx = g // 2, g % 2
                        q = slice(32 * g, 32 * g + 32)
                        src = nat[q, 1 - dy:1 - dy + PR + 1, 1 - dx:1 - dx + PR + 1]
                        sp.dma_start(shifted[q, 0:PR + 1, 0:PR + 1], src).then_inc(shift_in, 16)
                if kind == "OUT":
                    sp.wait_ge(out_made, m.at(1, 1))
                    for yl in range(YL):
                        src = ffn[PR * yl:PR * yl + PR, :, :].rearrange("p (a e) c -> p a (e c)", e=2)
                        sp.dma_start(rows_of(out, m, yl), src).then_inc(out_stored, 16)

            walk(sp, "sync", step)
            sp.wait_ge(out_stored, 16 * YL * B)

        @block.tensor
        def _(pe):
            eye = eye_center[:, 0:128]
            pe.wait_ge(eye_in, 16)
            def turn(t):
                for k in range(2):
                    pe.wait_ge(stage_in[k], t * 16 + 16)
                    for b in range(4):
                        wait(pe, stage_read, t * 8 + (4 * k + b - 3))
                        for j in range(TILES):
                            bank = 2 * b + (j >= 4)
                            dst = ps[:, bank, (j % 4) * PT:(j % 4 + 1) * PT]
                            mm = pe.transpose(dst, stage[k][:, b, j * 128:(j + 1) * 128], eye[0:PT, 0:PT])
                        mm.then_inc(stage_turned, 1)

            turn(0)
            with pe.Fori(1, 4) as t:
                turn(t)
            pe.wait_ge(consts_in, 16 * 24)
            pe.wait_ge(dve_pre, 1)
            pe.matmul(ps[:, 0, 0:B], mean4_sb[:, :], bw[:, 0, :], start=True, stop=True).then_inc(pe_pre, 1)
            pe.wait_ge(dve_pre, 2)
            pe.matmul(ps[:, 1, 0:B], mean4_sb[:, :], bw[:, 2, :], start=True, stop=True).then_inc(pe_pre, 1)
            for h in range(HEADS):
                pe.wait_ge(dve_pre, 3 + h)
                mm = pe.matmul(ps[:, 2, C * h:C * h + C], wvr[:, :] if h % 2 == 0 else xres[0:32, 128:256],
                               wd_s[:, C * h:C * h + C], start=True, stop=True)
                mm.then_inc(pe_pre, 1)

            def step(kind, m, n, rd):
                if rd:
                    slot, _, before = rd
                    o = ring(slot) if kind in RING else misc()
                    if before and not (kind == "DN" and n % 4):
                        k, image, r = before
                        pe.wait_ge(READ[k][0], image.at(READ[k][1], r + 1))
                if kind == "XT":
                    pe.wait_ge(x_in, m.at(64, 64))
                    for k in range(HALF[n]):
                        j = 4 * n + k
                        mm = pe.transpose(o[:, PT * k:PT * k + PT], xt[:, 128 * j:128 * j + 128], eye[0:PT, 0:PT])
                    mm.then_inc(misc_full, 1)
                elif kind == "CV":
                    pe.wait_ge(shift_in, m.at(64, 64))
                    w = HALF[n]
                    dst = o[:, 0:w * PT].rearrange("p (j y x) -> p j y x", j=w, y=YL)
                    for k in range(4):
                        di, dj = k // 2, k % 2
                        src = shifted[:, di:di + PR, dj:dj + PR].rearrange("p (y j) x -> p j y x", j=TILES)
                        mm = pe.matmul(dst, conv_w[:, k, :], src[:, 4 * n:4 * n + w], start=(k == 0), stop=(k == 3))
                    mm.then_inc(misc_full, 1)
                elif kind == "XC":
                    pe.wait_ge(t1_made, m.at(2, 2))
                    for j in range(TILES):
                        mm = pe.matmul(o[0:PT, j // 4, 128 * (j % 4):128 * (j % 4) + 128],
                                       t1[:, m.par, PT * j:PT * j + PT], eye_center[:, 128:256], start=True, stop=True)
                    mm.then_inc(ring_full, 1)
                elif kind in ("ZT", "ZU"):
                    ln = kind == "ZU"
                    pe.wait_ge(parts_made[ln], m.at(1, 1))
                    pe.wait_ge(eye16_made, 1)
                    of = o.bitcast(F16)
                    for k in range(14):
                        for q, w in (((0, 32), (32, 32), (64, 32), (96, 32)) if k == 0 else ((0, 64), (64, 64))):
                            mm = pe.matmul(of[q:q + w, k // 7, PT * (k % 7):PT * (k % 7) + PT],
                                           parts[ln][:, 14 * n + k, q % 64:q % 64 + w],
                                           eye16[0:PT, 0:PT], is_transpose=True, start=True, stop=True)
                    mm.then_inc(ring_full, 1)
                elif kind == "K":
                    pe.wait_ge(z_made[0], m.at(2, n // 7 + 1))
                    for k in range(2):
                        s = 2 * n + k
                        mm = pe.matmul(o[0:PT, k, :], z1[:, m.par, PT * s:PT * s + PT], wk16[:, :], start=True, stop=True)
                    mm.then_inc(ring_full, 1)
                elif kind == "KX":
                    pe.wait_ge(k_made, m.at(14, n + 1))
                    if n in (0, 7):
                        pe.wait_ge(xcs_made, m.at(2, n // 7 + 1))
                    if n == 0:
                        wait(pe, kt_copied, m.at(1))
                    for k in range(2):
                        mm = pe.matmul(kt_bank[64 * k:64 * k + 64, :],
                                       xcs[:, 2 * n + k, :, :].rearrange("p a c -> p (a c)"),
                                       kbuf[:, n % 2, DH * k:DH * k + DH], start=(n == 0), stop=(n == 13))
                    mm.then_inc(ktx_done, 1)
                elif kind == "G":
                    pe.wait_ge(kt_copied, m.at(1, 1))
                    for k in range(2):
                        c = 2 * n + k
                        mm = pe.matmul(o[:, k, 0:2 * HPC * 33], ktsb[:, 128 * c:128 * c + 128],
                                       p2[:, c, :, :, :].rearrange("p a h o -> p (a h o)"), start=True, stop=True)
                    mm.then_inc(ring_full, 1)
                elif kind == "Q":
                    j, k0 = n // 2, 2 * (n % 2)
                    for k in range(2):
                        mm = pe.matmul(o[:, k, 0:G * PT], wq16[:, 128 * (k0 + k):128 * (k0 + k) + 128],
                                       z1[:, m.par, G * PT * j:G * PT * (j + 1)], start=True, stop=True)
                    mm.then_inc(ring_full, 1)
                elif kind == "DN":
                    h, c = n // 4, n % 4
                    pe.wait_ge(q_made, m.at(14, 8 * h + 8 if h == 0 else 14))
                    if n == 0:
                        pe.wait_ge(g_made, m.at(2, 2))
                    for j in range(HALF[h]):
                        mm = pe.matmul(o[32 * j:32 * j + 32, 0:HW4],
                                       dmat[:, m.par, c, :, :].rearrange("p a h -> p (a h)"),
                                       qbuf[:, c, 4 * h + j, :], start=(c == 0), stop=(c == CH - 1))
                    if c == CH - 1:
                        mm.then_inc(misc_full, 1)
                elif kind == "SU":
                    pe.wait_ge(dcs_made, m.at(2, n + 1))
                    pe.matmul(o[:, 0:HW4], dsum_sb[:, :], dcs[:, :], start=True, stop=True).then_inc(misc_full, 1)
                elif kind == "R":
                    j, k0 = n // 2, 2 * (n % 2)
                    pe.wait_ge(r_made, m.at(2, 1 + j // 4))
                    for k in range(2):
                        a = 4 * (k0 + k) + j % 4
                        mm = pe.matmul(o[:, k, 0:HW4], sel16[:, 128 * a:128 * a + 128], rs[:, j // 4, :],
                                       start=True, stop=True)
                    mm.then_inc(ring_full, 1)
                elif kind == "NM":
                    pe.wait_ge(qr_made, m.at(14, 2 * n + 2))
                    for c in range(CH):
                        for v in range(2):
                            rhs = qbuf[:, c, n, :].rearrange("p (a v t) -> p a v t", a=2, v=2)[:, :, v, :]
                            mm = pe.matmul(o[64 * v:64 * v + 64, 0:2 * PT].rearrange("p (a t) -> p a t", a=2),
                                           gmat[:, m.par, c, :, :].rearrange("p a o -> p (a o)"), rhs,
                                           start=(c == 0), stop=(c == CH - 1))
                    mm.then_inc(misc_full, 1)
                elif kind == "T2":
                    tiles = range(2 * n, min(2 * n + 2, TILES))
                    pe.wait_ge(numer_made, m.at(7, tiles[-1] + 1))
                    if n == 0:
                        pe.wait_ge(t1b_made, m.at(1, 1))
                    for jj, j in enumerate(tiles):
                        dst = o[0:PT, 256 * jj:256 * jj + 256]
                        pe.matmul(dst, t1b[:, PT * j:PT * j + PT], eye_center[:, :], start=True, stop=False)
                        for a in range(2):
                            mm = pe.matmul(dst.rearrange("p (q a c) -> p q a c", q=2, a=2)[:, :, a, :],
                                           pbuf[:, j % 4, a, :], pair_sb[:, :].rearrange("p (q c) -> p q c", q=2),
                                           start=False, stop=(a == 1))
                    mm.then_inc(misc_full, 1)
                elif kind == "LG":
                    pe.wait_ge(z_made[1], m.at(2, 2))
                    for s in range(SLOTS):
                        mm = pe.matmul(o[0:PT, 0, EXPERTS * s:EXPERTS * s + EXPERTS], z2[:, PT * s:PT * s + PT],
                                       we16[:, EXPERTS * C:], start=True, stop=True)
                    mm.then_inc(ring_full, 1)
                elif kind == "F":
                    for k in range(4):
                        s = 4 * n + k
                        mm = pe.matmul(o[0:PT, k // 2, 256 * (k % 2):256 * (k % 2) + 256], z2[:, PT * s:PT * s + PT],
                                       we16[:, 0:EXPERTS * C], start=True, stop=True)
                    mm.then_inc(ring_full, 1)

            pe.wait_ge(dve_pre, 22)
            walk(pe, "tensor", step)

        @block.scalar
        def _(act):
            act.wait_ge(dve_pre, 19)
            for v in range(2):
                for cs in range(2):
                    q = slice(64 * v + 32 * cs, 64 * v + 32 * cs + 32)
                    dst = p2[q, :, cs, :, 0:C]
                    last = act.activation(dst, ps[q, 2, :].rearrange("p (a h o) -> p a h o", a=CH, h=HPC), ACT.Copy,
                                          scale=SHIFT)
            last.then_inc(act_pre, 1)
            act.wait_ge(dve_pre, 22)

            def step(kind, m, n, rd):
                if rd:
                    slot, no, _ = rd
                    o = ring(slot) if kind in RING else misc()
                if kind == "XT":
                    act.wait_ge(binarized, m.at(2, n + 1))
                    if n == 0:
                        wait(act, t1_made, m.at(2))
                    a, b = COL[n]
                    act.activation(xres[:, a:b], o[:, 0:b - a], ACT.Identity, bias=conv_bias).then_inc(xres_made, 1)
                elif kind == "XC":
                    act.wait_ge(ring_full, no + 1)
                    wait(act, xn_made[0], m.at(1))
                    wait(act, ssum_made[0], m.at(1))
                    for k in range(2):
                        a, w = 16 * k, 4 * HALF[k]
                        src = o[0:PT, k, 0:w * C].rearrange("p (s c) -> p s c", c=C)
                        act.activation(xc[0][:, a:a + w, :], src, ACT.Copy)
                        last = act.activation(sq1[:, a:a + w, :], src, ACT.Square)
                    last.then_inc(xc_made[0], 1)
                elif kind in ("XH1", "XH2"):
                    ln = kind == "XH2"
                    act.wait_ge(xn_made[ln], m.at(1, 1))
                    act.activation(parts[ln][:, :, 0:C], xn[ln][:, :, :], ACT.Copy).then_inc(high_made[ln], 1)
                elif kind in ("ZT", "ZU"):
                    ln = kind == "ZU"
                    act.wait_ge(ring_full, no + 1)
                    if ln and n == 0:
                        wait(act, prod_made, m.at(7))
                    dst = (z2 if ln else z1[:, m.par, :])[:, 14 * PT * n:14 * PT * (n + 1)]
                    act.activation(dst.rearrange("p (a b) -> p a b", a=2), o.bitcast(F16)[:, :, 0:7 * PT], ACT.Copy)\
                        .then_inc(z_made[ln], 1)
                elif kind == "K":
                    act.wait_ge(ring_full, no + 1)
                    wait(act, k_made, m.at(14, n))
                    act.activation(ebuf[0:PT, 0, :].rearrange("p (a b) -> p a b", a=2), o[0:PT, :, :], ACT.Exp,
                                   bias=minus_one[0:PT, :]).then_inc(kexp_made, 1)
                elif kind == "Q":
                    act.wait_ge(ring_full, no + 1)
                    wait(act, q_made, m.at(14, n))
                    act.activation(ebuf[:, 1, 0:2 * G * PT].rearrange("p (a b) -> p a b", a=2), o[:, :, 0:G * PT],
                                   ACT.Exp, bias=minus_one).then_inc(qexp_made, 1)
                elif kind == "KT":
                    act.wait_ge(ktx_done, m.at(14, 14))
                    act.activation(ktsb[:, :], kt_bank, ACT.Copy).then_inc(kt_copied, 1)
                elif kind == "G":
                    act.wait_ge(ring_full, no + 1)
                    src = o[:, :, 0:2 * HPC * 33].rearrange("p k (a h o) -> p k a h o", a=2, h=HPC)
                    wait(act, numer_made, m.at(7, -7))
                    for h in range(HPC):
                        q = slice(32 * h, 32 * h + 32)
                        act.activation(gmat[q, m.par, 2 * n:2 * n + 2, :, :], src[q, :, :, h, 0:C], ACT.Copy)
                        for k in range(2):
                            c = 2 * n + k
                            last = act.activation(dmat[q, m.par, c, :, HPC * c + h], src[q, k, :, h, C], ACT.Copy)
                    last.then_inc(g_made, 1)
                elif kind == "SU":
                    act.wait_ge(misc_full, no + 1)
                    wait(act, r_made, m.at(2, n))
                    act.activation(den[:, :], o[:, 0:HW4], ACT.Identity, bias=den_eps).then_inc(den_made, 1)
                elif kind == "T2":
                    act.wait_ge(misc_full, no + 1)
                    if n == 0:
                        wait(act, out_made, m.at(1, -1))
                        wait(act, xn_made[1], m.at(1))
                    wait(act, piece_summed, m.at(4, n - 1))
                    w = min(2, TILES - 2 * n)
                    src = o[0:PT, 0:256 * w].rearrange("p (j q f) -> p j q f", j=w, q=2)
                    cen = src[:, :, 1, :].rearrange("p j (g c) -> p j g c", g=G)
                    a = 2 * n
                    act.activation(t2[:, m.par, 128 * a:128 * (a + w)].rearrange("p (j f) -> p j f", j=w), src[:, :, 0, :],
                                   ACT.Copy)
                    sl = slice(G * a, G * (a + w))
                    act.activation(xc[1][:, sl, :].rearrange("p (j g) c -> p j g c", j=w), cen, ACT.Copy)
                    act.activation(sq2[:, n % 2, 0:4 * w, :].rearrange("p (j g) c -> p j g c", j=w), cen, ACT.Square)\
                        .then_inc(t2_made, 1)
                elif kind == "TB":
                    act.wait_ge(t1_made, m.at(2, 2))
                    act.activation(t1b[:, :], t1[:, m.par, :], ACT.Identity, bias=dense_b).then_inc(t1b_made, 1)
                elif kind == "RT" and n == 5:
                    act.wait_ge(route_step, m.at(18, 13))
                    act.activation(rmax[:, 3, :], rmax[:, 2, :], ACT.Exp).then_inc(ratio_made, 1)

            walk(act, "scalar", step)

        @block.gpsimd
        def _(pool):
            nc.gpsimd.memset(power[:, :], -0.5).then_inc(pool_pre, 1)
            pool.wait_ge(pool_pre, 1)
            pool.wait_ge(dve_pre, 20)
            nc.gpsimd.tensor_tensor(bw[:, 4, :], bw[:, 3, :], power[:, :], ALU.pow).then_inc(pool_pre, 1)
            pool.wait_ge(dve_pre, 21)
            nc.gpsimd.tensor_tensor(bn_inv, bn_half, power[:, 0:1], ALU.pow).then_inc(pool_pre, 1)

            def step(kind, m, n, rd):
                if kind in ("PN1", "PN2"):
                    ln = kind == "PN2"
                    pool.wait_ge(var_made[ln], m.at(1, 1))
                    nc.gpsimd.tensor_tensor(rstd[ln][:, :], varr[ln][:, :], power[0:PT, 0:SLOTS], ALU.pow)\
                        .then_inc(rstd_made[ln], 1)
                    pool.wait_ge(rstd_made[ln], m.at(1, 1))
                    wait(pool, high_made[ln], m.at(1))
                    nc.gpsimd.tensor_tensor(xn[ln][:, :, 0:C - 1], xc[ln][:, :, 0:C - 1],
                                            rstd[ln][:, :].unsqueeze(2).to_broadcast([PT, SLOTS, C - 1]), ALU.mult)\
                        .then_inc(xn_made[ln], 1)
                elif kind in ("PL1", "PL2"):
                    ln = kind == "PL2"
                    pool.wait_ge(high_made[ln], m.at(1, 1))
                    nc.gpsimd.tensor_tensor(parts[ln][:, :, C:2 * C], xn[ln][:, :, :], parts[ln][:, :, 0:C],
                                            ALU.subtract).then_inc(parts_made[ln], 1)
                elif kind == "CS":
                    pool.wait_ge(xn_made[0], m.at(1, 1))
                    wait(pool, ktx_done, m.at(14, 7 * n - 7))
                    w = slice(14 * n, 14 * n + 14)
                    for k in range(2):
                        last = nc.gpsimd.tensor_tensor(xcs[:, w, k, :], xn[0][:, w, :],
                                                       tabk[:, k, w].unsqueeze(2).to_broadcast([PT, 14, C]), ALU.mult)
                    last.then_inc(xcs_made, 1)
                elif kind == "F":
                    pool.wait_ge(prod_made, m.at(7, n + 1))
                    if n == 0:
                        wait(pool, out_stored, m.at(64))
                    p = prod[:, n % 2, :, :]
                    nc.gpsimd.tensor_tensor(p[:, :, 0:4 * C], p[:, :, 0:4 * C], p[:, :, 4 * C:], ALU.add)\
                        .then_inc(pool_add, 1)
                    pool.wait_ge(pool_add, m.at(14, 2 * n + 1))
                    nc.gpsimd.tensor_tensor(p[:, :, 0:2 * C], p[:, :, 0:2 * C], p[:, :, 2 * C:4 * C], ALU.add)\
                        .then_inc(pool_add, 1)
                    pool.wait_ge(pool_add, m.at(14, 2 * n + 2))
                    nc.gpsimd.tensor_tensor(ffn[:, 4 * n:4 * n + 4, :], p[:, :, 0:C], p[:, :, C:2 * C], ALU.add)\
                        .then_inc(ffn_made, 1)

            walk(pool, "gpsimd", step)

        @block.vector
        def _(dve):
            own = [0]
            chain = sem("chain")

            def link(ins):
                own[0] += 1
                ins.then_inc(chain, 1)
                dve.wait_ge(chain, own[0])

            v = nc.vector
            v.memset(minus_one, -1.0)
            v.memset(den_eps, DEN_EPS * SHIFT)
            v.memset(nat[:, :, :], 1.0)
            v.memset(dmat[:, :, :, :, :], 0.0)
            for ln in range(2):
                link(v.memset(xn[ln][:, :, C - 1:C], 1.0))
            with dve.Fori(0, 4) as t:
                for k in range(2):
                    for b in range(4):
                        img = t * 8 + (4 * k + b)
                        dve.wait_ge(stage_turned, img + 1)
                        for h in range(2):
                            last = v.bn_stats(stats[:, bass.ds(img, 1), 6 * h:6 * h + 6].rearrange("p a k -> p (a k)"),
                                              ps[:, 2 * b + h, 0:HALF[h] * PT])
                        last.then_inc(stage_read, 1)
            dve.wait_ge(stage_read, B)
            dve.wait_ge(consts_in, 16 * 24)
            for b in range(B):
                last = v.bn_aggr(mv[:, b, :], stats[:, b, :])
            link(last)
            v.tensor_copy(bw[:, 0, :], mv[:, :, 0]).then_inc(dve_pre, 1)
            dve.wait_ge(pe_pre, 1)
            link(v.tensor_copy(bw[:, 1, :], ps[:, 0, 0:B]))
            link(v.tensor_tensor(bw[:, 5, :], mv[:, :, 0], bw[:, 1, :], ALU.subtract))
            link(v.tensor_tensor(bw[:, 6, :], bw[:, 5, :], bw[:, 5, :], ALU.mult))
            v.tensor_tensor(bw[:, 2, :], mv[:, :, 1], bw[:, 6, :], ALU.add).then_inc(dve_pre, 1)
            link(v.tensor_tensor(wva_s, wva_s, wvb_s, ALU.subtract))
            for h in range(HEADS):
                if h >= 2:
                    dve.wait_ge(pe_pre, 2 + h - 1)
                o = 128 * (h % 2)
                v.tensor_copy(xres[0:32, o:o + 128].rearrange("p (k a) -> p k a", k=4),
                              wva_s[:, C * h:C * h + C].unsqueeze(1).to_broadcast([32, 4, C])).then_inc(dve_pre, 1)
            dve.wait_ge(pe_pre, 2 + HEADS)
            v.tensor_scalar(minus_one, minus_one, 1.0, None, ALU.mult).then_inc(dve_pre, 1)
            link(v.tensor_scalar(bw[:, 3, :], ps[:, 1, 0:B], GN_EPS, None, ALU.add))
            link(v.tensor_copy(bw[:, 7, :], ps[:, 1, 0:B]))
            v.tensor_copy(small[:, 12:13], small[:, 0:1]).then_inc(dve_pre, 1)
            dve.wait_ge(pool_pre, 2)
            link(v.tensor_tensor(bw[:, 5, :], bw[:, 7, :], bw[:, 4, :], ALU.mult))
            link(v.tensor_tensor(bw[:, 6, :], bw[:, 5, :], bw[:, 4, :], ALU.mult))
            link(v.tensor_reduce(bn_gain, bw[:, 6, :], AX_X, ALU.add))
            v.tensor_scalar(bn_half, bn_gain, 1.0 / B, BN_EPS, ALU.mult, ALU.add).then_inc(dve_pre, 1)
            dve.wait_ge(pool_pre, 3)
            link(v.tensor_tensor(bn_gain, bn_inv, gamma_c, ALU.mult))
            link(v.tensor_scalar(bin_a[:, :], bw[:, 4, :], bn_gain, None, ALU.mult))
            link(v.tensor_tensor(bw[:, 5, :], bin_a[:, :], bw[:, 1, :], ALU.mult))
            link(v.tensor_scalar(bin_thr[:, :], bw[:, 5, :], beta_c, None, ALU.subtract))
            rows, rows2, tmp = views["rows"], views["rows2"], views["tmp"]
            link(v.tensor_scalar(rows2, rows, -1.0, None, ALU.mult))
            link(v.tensor_tensor(rows2, rows2, rows, ALU.max))
            link(v.tensor_reduce(conv_scale, rows2, AX_X, ALU.add))
            link(v.tensor_scalar(conv_scale, conv_scale, 1.0 / (9 * C), None, ALU.mult))
            link(v.tensor_scalar(rows2, rows, 0.0, 2.0, ALU.is_ge, ALU.mult))
            link(v.tensor_scalar(rows2, rows2, -1.0, None, ALU.add))
            link(v.tensor_reduce(conv_sum, rows2, AX_X, ALU.add))
            link(v.tensor_tensor(conv_bias, conv_scale, conv_sum, ALU.mult))
            link(v.tensor_scalar(conv_bias, conv_bias, -1.0, None, ALU.mult))
            link(v.tensor_scalar(conv_scale2, conv_scale, 2.0, None, ALU.mult))
            link(v.tensor_scalar(tmp, views["taps"], 0.0, 2.0, ALU.is_ge, ALU.mult))
            link(v.tensor_scalar(tmp, tmp, -1.0, None, ALU.add))
            link(v.tensor_tensor(conv_w[:, :, :].rearrange("p a b -> p (a b)"), tmp, views["valid"], ALU.mult))
            for dst, a, b, w in ((wq16, views["wqa"], wqb_s, DH), (wk16, views["wka"], wkb_s, DH),
                                 (we16, views["wea"], web_s, 264)):
                link(v.tensor_tensor(a, a, b, ALU.subtract))
                link(v.tensor_copy(dst[:, 0:w], a))
                link(v.tensor_tensor(dst[64:128, 0:w], a[64:128], dst[64:128, 0:w], ALU.subtract))
            v.tensor_copy(eye16[:, :], eye_center[:, 0:128]).then_inc(eye16_made, 1)
            link(v.tensor_copy(sel16[:, :], views["sel"]))
            dve.wait_ge(act_pre, 1)
            v.tensor_copy(small[:, 12:13], small[:, 0:1]).then_inc(dve_pre, 1)

            def step(kind, m, n, rd):
                if rd:
                    slot, no, _ = rd
                    o = ring(slot) if kind in RING else misc()
                if kind == "XT":
                    dve.wait_ge(misc_full, no + 1)
                    if n == 0:
                        wait(dve, shift_in, m.at(64))
                    w = HALF[n]
                    dst = nat[:, 1:1 + PR, 1:1 + PR].rearrange("p (y j) x -> p j y x", j=TILES)[:, 4 * n:4 * n + w]
                    i = bass.ds(m.at(1), 1) if m.t is not None else slice(m.c, m.c + 1)
                    for y in range(YL):
                        last = v.tensor_scalar(dst[:, :, y, :],
                                               o[:, 0:w * PT].rearrange("p (j y x) -> p j y x", j=w, y=YL)[:, :, y, :],
                                               bin_a[:, i], bin_thr[:, i], ALU.mult, ALU.is_ge)
                    last.then_inc(binarized, 1)
                elif kind == "CV":
                    dve.wait_ge(misc_full, no + 1)
                    dve.wait_ge(xres_made, m.at(2, n + 1))
                    if n == 0:
                        wait(dve, t1b_made, m.at(1, -1))
                    a, b = COL[n]
                    v.scalar_tensor_tensor(t1[:, m.par, a:b], o[:, 0:b - a], conv_scale2, xres[:, a:b], ALU.mult,
                                           ALU.add).then_inc(t1_made, 1)
                elif kind in ("SM1", "SM2"):
                    ln = kind == "SM2"
                    if ln:
                        dve.wait_ge(piece_summed, m.at(4, 4))
                    else:
                        dve.wait_ge(xc_made[0], m.at(1, 1))
                        v.tensor_reduce(ssum[0][:, :], sq1[:, :, :], AX_X, ALU.add).then_inc(ssum_made[0], 1)
                        dve.wait_ge(ssum_made[0], m.at(1, 1))
                    wait(dve, rstd_made[ln], m.at(1))
                    v.tensor_scalar(varr[ln][:, :], ssum[ln][:, :], 1.0 / C, LN_EPS, ALU.mult, ALU.add)\
                        .then_inc(var_made[ln], 1)
                elif kind == "T2":
                    dve.wait_ge(t2_made, m.at(4, n + 1))
                    w = G * min(2, TILES - 2 * n)
                    v.tensor_reduce(ssum[1][:, 2 * G * n:2 * G * n + w], sq2[:, n % 2, 0:w, :], AX_X, ALU.add)\
                        .then_inc(piece_summed, 1)
                elif kind == "K":
                    dve.wait_ge(kexp_made, m.at(14, n + 1))
                    wait(dve, ktx_done, m.at(14, n - 1))
                    v.scalar_tensor_tensor(kbuf[:, n % 2, :].rearrange("p (a b) -> p a b", a=2), o[0:PT, :, :], 1.0,
                                           ebuf[0:PT, 0, :].rearrange("p (a b) -> p a b", a=2), ALU.max, ALU.min)\
                        .then_inc(k_made, 1)
                elif kind == "Q":
                    j, k0 = n // 2, 2 * (n % 2)
                    dve.wait_ge(qexp_made, m.at(14, n + 1))
                    v.scalar_tensor_tensor(qbuf[:, k0:k0 + 2, j, :], o[:, :, 0:G * PT], 1.0,
                                           ebuf[:, 1, 0:2 * G * PT].rearrange("p (a b) -> p a b", a=2), ALU.max,
                                           ALU.min).then_inc(q_made, 1)
                elif kind == "DN" and n % 4 == 3:
                    h = n // 4
                    dve.wait_ge(misc_full, no + 1)
                    wait(dve, den_made, m.at(2, h))
                    q = slice(0, 32 * HALF[h])
                    v.tensor_tensor(dcs[q, :], o[q, 0:HW4], tabd[q, h, :], ALU.mult).then_inc(dcs_made, 1)
                elif kind == "RC":
                    dve.wait_ge(den_made, m.at(2, n + 1))
                    v.reciprocal(den[:, :], den[:, :]).then_inc(recip_made, 1)
                    dve.wait_ge(recip_made, m.at(2, n + 1))
                    v.tensor_copy(rs[:, n, :], den[:, :]).then_inc(rhigh_made, 1)
                    dve.wait_ge(rhigh_made, m.at(2, n + 1))
                    v.tensor_tensor(rs[64:128, n, :], den[64:128, :], rs[64:128, n, :], ALU.subtract)\
                        .then_inc(r_made, 1)
                elif kind == "R":
                    j, k0 = n // 2, 2 * (n % 2)
                    dve.wait_ge(ring_full, no + 1)
                    v.tensor_tensor(qbuf[:, k0:k0 + 2, j, :], o[:, :, 0:G * PT], qbuf[:, k0:k0 + 2, j, :], ALU.mult)\
                        .then_inc(qr_made, 1)
                elif kind == "NM":
                    dve.wait_ge(misc_full, no + 1)
                    wait(dve, t2_made, m.at(4, (n - 4) // 2 + 1 if n >= 4 else 0))
                    v.tensor_tensor(pbuf[:, n % 4, :, :].rearrange("p a t -> p (a t)"), o[:, 0:2 * PT],
                                    tabn[:, n, :], ALU.mult).then_inc(numer_made, 1)
                elif kind == "LG":
                    dve.wait_ge(ring_full, no + 1)
                    v.tensor_copy(route[:, 0, :], o[0:PT, 0, 0:SLOTS * EXPERTS]).then_inc(route_step, 1)
                elif kind == "RT":
                    shape = [PT, SLOTS, EXPERTS]

                    def grid(a):
                        return a.rearrange("p (s e) -> p s e", e=EXPERTS)

                    def spread(a):
                        return a.unsqueeze(2).to_broadcast(shape)

                    logits, hot1, hot2, rest = (route[:, k, :] for k in range(4))
                    top1, top2, diff, ratio, w1, w2 = (rmax[:, k, :] for k in range(6))

                    def after(k):
                        dve.wait_ge(route_step, m.at(18, k))

                    if n in (0, 3):
                        top, src, hot, w, k = (top1, logits, hot1, w1, 1) if n == 0 else (top2, rest, hot2, w2, 7)
                        after(k)
                        v.tensor_reduce(top, grid(src), AX_X, ALU.max).then_inc(route_step, 1)
                        after(k + 1)
                        v.tensor_tensor(grid(hot), grid(src), spread(top), ALU.is_equal).then_inc(route_step, 1)
                    elif n in (1, 4):
                        hot, w, k = (hot1, w1, 3) if n == 1 else (hot2, w2, 9)
                        after(k)
                        v.tensor_tensor(hot, hot, first[:, :], ALU.mult).then_inc(route_step, 1)
                        after(k + 1)
                        v.tensor_reduce(w, grid(hot), AX_X, ALU.max).then_inc(route_step, 1)
                    elif n == 2:
                        after(5)
                        v.tensor_tensor(grid(hot1), grid(hot1), spread(w1), ALU.is_equal).then_inc(route_step, 1)
                        after(6)
                        v.scalar_tensor_tensor(rest, hot1, -3.0e38, logits, ALU.mult, ALU.add).then_inc(route_step, 1)
                    elif n == 5:
                        after(11)
                        v.tensor_tensor(grid(hot2), grid(hot2), spread(w2), ALU.is_equal).then_inc(route_step, 1)
                        v.tensor_tensor(diff, top2, top1, ALU.subtract).then_inc(route_step, 1)
                    elif n == 6:
                        dve.wait_ge(ratio_made, m.at(1, 1))
                        v.tensor_scalar(w1, ratio, 1.0, None, ALU.add).then_inc(route_step, 1)
                        after(14)
                        v.reciprocal(w2, w1).then_inc(route_step, 1)
                        after(15)
                        v.tensor_tensor(w1, ratio, w2, ALU.mult).then_inc(route_step, 1)
                        v.tensor_tensor(grid(hot1), grid(hot1), spread(w2), ALU.mult).then_inc(route_step, 1)
                        after(16)
                        v.tensor_tensor(grid(hot2), grid(hot2), spread(w1), ALU.mult).then_inc(route_step, 1)
                        after(18)
                        v.tensor_tensor(gate[:, :], hot1, hot2, ALU.add).then_inc(gate_made, 1)
                elif kind == "F":
                    dve.wait_ge(ring_full, no + 1)
                    if n == 0:
                        dve.wait_ge(gate_made, m.at(1, 1))
                    wait(dve, ffn_made, m.at(7, max(n - 1, 0)))
                    w = 4 * EXPERTS
                    v.tensor_tensor(prod[:, n % 2, :, :].rearrange("p s (e c) -> p (s e) c", c=C),
                                    o[0:PT, :, :].rearrange("p k (s c) -> p (k s) c", c=C),
                                    gate[:, w * n:w * n + w].unsqueeze(2).to_broadcast([PT, w, C]), ALU.mult)\
                        .then_inc(prod_made, 1)
                elif kind == "OUT":
                    dve.wait_ge(ffn_made, m.at(7, 7))
                    f = ffn[:, :, :].rearrange("p s c -> p (s c)")
                    v.tensor_tensor(f, f, t2[:, m.par, :], ALU.add).then_inc(out_made, 1)

            walk(dve, "vector", step)


def kernel(**inputs):
    import numpy as _np
    import concourse.bacc as _bacc
    from concourse import mybir as _mybir
    from concourse.bass_utils import run_bass_kernel_spmd as _run

    get = {k: _np.ascontiguousarray(v) for k, v in inputs.items()}
    f = _np.float32

    def column(a):
        return _np.ascontiguousarray(_np.tile(a, G)[:, None])

    def folded(w, b, const, copies):
        n = w.shape[1]
        a = _np.concatenate([w[0:C - 1], b[None, :]], 0)
        r = _np.concatenate([_np.tile(w[C - 1:C], (C - 1, 1)), _np.full((1, n), const, f)], 0)
        return _np.stack([_np.tile(a, (copies, 1)), _np.tile(r, (copies, 1))])

    conv = get["L0_conv_W"]
    taps = _np.zeros((G, C, 2, 2, G, C), f)
    for kh, kw, gi, i, j, go in _taps():
        taps[gi, :, i, j, go, :] = conv[kh, kw]
    rows = _np.tile(conv.reshape(9 * C, C).T, (G, 1))
    wq = folded(get["L1_attn_wq_w"].T, get["L1_attn_wq_b"], -1.0, 4)
    wk = folded(get["L1_attn_wk_w"].T, get["L1_attn_wk_b"], -1.0, 4)
    wv = folded(get["L1_attn_wv_w"].T, get["L1_attn_wv_b"], 0.0, 1)
    wv = wv.reshape(2, C, HEADS, C).transpose(0, 3, 2, 1).reshape(2, C, DH)
    wd = get["L1_attn_dense_w"].reshape(C, HEADS, C).transpose(2, 1, 0).reshape(C, DH)
    expert = get["L1_ffn_expert_w"].transpose(1, 0, 2).reshape(C, EXPERTS * C)
    we = folded(_np.concatenate([expert, get["L1_ffn_router_w"]], 1),
                _np.concatenate([get["L1_ffn_expert_b"].reshape(-1), get["L1_ffn_router_b"]]), 0.0, 4)
    c = consts()
    arrays = dict(x=get["x"], gamma=column(get["L0_conv_gamma"]), beta=column(get["L0_conv_beta"]),
                  conv_taps=taps.reshape(128, 512), conv_rows=rows, wq=wq, wk=wk, wv=wv, wd=wd,
                  wd_b=column(get["L1_attn_dense_b"]), we=we, eyec=c["eyec"], mean4=c["mean4"], pair=c["pair"],
                  dsum=c["dsum"], sel=c["sel"], p2c=c["p2"], tabdc=c["tabd"], tabnc=c["tabn"], tabkc=c["tabk"],
                  firstc=c["first"], validc=c["valid"])
    nc = _bacc.Bacc("TRN2", target_bir_lowering=False, num_devices=1)
    arrays = {k: _np.ascontiguousarray(a) for k, a in arrays.items()}
    args = {k: nc.dram_tensor(f"in_{k}", a.shape, _mybir.dt.from_np(a.dtype), kind="ExternalInput").ap()
            for k, a in arrays.items()}
    out = nc.dram_tensor("out_0", (B, HW, HW, C), F32, kind="ExternalOutput").ap()
    build(nc, out=out, **args)
    r = _run(nc, [{f"in_{k}": a for k, a in arrays.items()}], core_ids=[0])
    return r.results[0]["out_0"]
```

```python
from contextlib import ExitStack

import concourse.bass as bass
import numpy as np
from concourse import mybir

F32 = mybir.dt.float32
F16 = mybir.dt.float16
BF16 = mybir.dt.bfloat16
ALU = mybir.AluOpType
ACT = mybir.ActivationFunctionType
AX_X = mybir.AxisListType.X

B, HW, C = 32, 56, 32
HEADS, EXPERTS = 16, 8
PR = HW // 2
G = 4
TILES = 7
YL = PR // TILES
PT = YL * PR
SLOTS = TILES * G
PATCHES = TILES * PT
TOKENS = HW * HW
DH = HEADS * C
CH = DH // 128
HPC = HEADS // CH
PITCH = PR + 2
HALF = (4, 3)
COL = [(0, 4 * PT), (4 * PT, 7 * PT)]
HW4 = G * PT
HALFW = HW4 // 2
LN_EPS, GN_EPS, BN_EPS = 1e-5, 1e-5, 1e-3
DEN_EPS = 1e-5
SHIFT = 2.0 ** -22


def consts():
    eye = np.eye(128, dtype=np.float32)
    i32 = np.eye(32, dtype=np.float32)
    center = np.kron(np.eye(4), i32 - 1.0 / 32).astype(np.float32)
    mean4 = np.kron(np.ones((4, 4)), i32 / 4).astype(np.float32)
    plain_mean = np.concatenate([np.eye(64), np.kron(np.eye(2), np.full((32, 1), 1.0 / 32))], 1)
    eye_mean = np.kron(np.eye(2), plain_mean).astype(np.float32)
    pair = plain_mean.reshape(2, 1, 32, 66).repeat(2, 1).reshape(128, 66).astype(np.float32)
    dsum = np.kron(np.eye(4), np.kron(np.ones((2, 1)), np.eye(16)))
    dsum = dsum.astype(np.float32)
    sel = np.zeros((2, 4, HEADS, CH, 4, HPC, 32), np.float32)
    for j in range(4):
        for h in range(HEADS):
            sel[:, j, h, h // HPC, j, h % HPC, :] = 1.0
    p2 = np.zeros((2, 2, 32, CH, 2, HPC, 33), np.float32)
    for cs in range(2):
        p2[:, cs, 31, :, cs, :, 32] = SHIFT
    tile, g, yl, px = np.meshgrid(np.arange(TILES), np.arange(G), np.arange(YL), np.arange(PR), indexing="ij")
    row, col = 2 * (TILES * yl + tile) + g // 2, 2 * px + g % 2
    s = (row * HW + col).reshape(TILES, G, PT)
    pos = np.float32(1.57) * np.arange(TOKENS, dtype=np.float32) / np.float32(TOKENS)
    cs = np.stack([np.cos(pos), np.sin(pos)]).astype(np.float32)[:, s]
    tabd = np.zeros((4, 2, HEADS, 2, HW4), np.float32)
    for j in range(TILES):
        tabd[j % 4, :, :, j // 4] = cs[:, j].reshape(2, 1, HW4)
    v = cs.reshape(2, TILES, 2, 2, PT)
    tabn = np.repeat(v.transpose(3, 0, 1, 2, 4)[:, :, None], 32, 2).reshape(128, 2 * PATCHES)
    tabk = cs.transpose(3, 0, 1, 2).reshape(PT, 2 * SLOTS)
    first = np.tile(np.arange(EXPERTS, 0, -1, dtype=np.float32), (PT, SLOTS))
    valid = np.zeros((G, 32, 2, 2, G, 32), np.float32)
    for (di, dj, gi, i, j, go) in _taps():
        valid[gi, :, i, j, go, :] = 1.0
    return dict(eyec=np.concatenate([eye, center], 1), eyem=eye_mean, mean4=mean4, pair=pair, dsum=dsum,
                sel=sel.reshape(128, -1), p2=p2.reshape(128, -1), tabd=tabd.reshape(128, -1), tabn=tabn, tabk=tabk,
                first=first, valid=valid.reshape(128, -1))


def _taps():
    for gi in range(G):
        for go in range(G):
            for i in range(2):
                for j in range(2):
                    kh = 2 * i + 1 - gi // 2 - go // 2
                    kw = 2 * j + 1 - gi % 2 - go % 2
                    if 0 <= kh <= 2 and 0 <= kw <= 2:
                        yield kh, kw, gi, i, j, go


class Img:

    def __init__(self, t, c):
        self.t, self.c = t, c

    def at(self, per, off=0):
        return self.c * per + off if self.t is None else self.t * (2 * per) + (self.c * per + off)

    @property
    def par(self):
        return self.c % 2


PERIOD = 14
RING_SLOTS = 3
RING = ("K", "R", "RP", "Q", "G", "LG", "F", "XC", "ZT", "ZU")
MISC = ("XT", "CV", "DN", "SU", "NM", "T2")


def schedule():
    s = []

    def add(kind, times):
        s.extend((t, kind, n) for n, t in enumerate(times))

    add("XT", [-23.13, -22.48])
    add("CV", [-13.11, -12.76])
    add("XC", [-9.58])
    add("SM1", [-7.96])
    add("PN1", [-9.24])
    add("XH1", [-6.50])
    add("PL1", [-9.21])
    add("CS", [-6.97, -6.70])
    add("ZT", [-5.63, -1.39])
    add("K", [-3.29, -2.86, -1.80, -0.32, 1.58, 1.92, 2.48, 3.24, 3.92, 4.87, 5.09, 5.90, 6.46, 6.99])
    add("KX", [-2.14, -1.87, 0.27, 1.02, 1.92, 3.45, 3.85, 4.93, 5.21, 5.42, 5.94, 7.03, 7.90, 8.06])
    add("KT", [8.36])
    add("G", [9.46, 9.86])
    add("Q", [4.11, 4.96, 5.65, 6.06, 6.46, 7.66, 8.18, 9.13, 11.09, 11.34, 11.83, 13.42, 14.97, 15.59])
    add("DN", [11.12, 11.19, 11.42, 11.50, 16.30, 16.54, 16.56, 16.68])
    add("SU", [12.02, 17.39])
    add("RC", [12.07, 17.64])
    add("RL", [13.24, 18.20])
    add("R", [14.96, 15.05, 15.84, 16.71, 19.33, 20.27, 24.24])
    add("RP", [13.85, 14.97, 15.97, 17.79, 18.78, 21.48, 23.54])
    add("NM", [15.85, 18.60, 20.07, 20.58, 22.99, 23.72, 26.77])
    add("TB", [15.28])
    add("T2", [21.90, 24.63, 24.96, 27.84])
    add("S2", [24.40, 27.26, 27.43, 29.55])
    add("SM2", [29.73])
    add("PN2", [27.61])
    add("XH2", [31.86])
    add("PL2", [30.69])
    add("ZU", [33.29, 33.68])
    add("LG", [34.09])
    add("RT", [34.52, 34.80, 35.84, 36.19, 36.22, 36.95, 37.18])
    add("GT", [35.17])
    add("F", [37.89, 38.65, 39.01, 39.68, 40.71, 42.71, 44.87])
    add("OUT", [46.76])
    return sorted(s)


SCHEDULE = schedule()
SHIFTS = {
    "tensor": {},
    "vector": {"CV": 0.27, "DN": 0.11, "F": 0.17, "K": 0.2, "LG": 0.19, "NM": 0.17, "Q": 0.21, "R": 0.19,
               "XT": 0.19},
    "scalar": {"G": 0.24, "K": 0.32, "Q": 0.32, "RC": 1.16, "RP": 0.33, "RT": -0.02, "S2": -0.19, "SU": 0.2,
               "T2": 0.23, "XC": 0.43, "XT": 0.61, "ZT": 0.16, "ZU": 0.55},
    "gpsimd": {"F": -2.19, "RP": -1.61, "T2": -1.77},
    "sync": {"CV": 5.7, "OUT": 3.11, "XT": -9.83},
}
LOOP_FIRST, LOOP_LAST = 3, B - 4


def iteration(engine, i):
    shift = SHIFTS[engine]
    steps = sorted((t + shift.get(kind, 0), t, kind, n) for t, kind, n in SCHEDULE)
    out = []
    for t, t0, kind, n in steps:
        d = int(t // PERIOD)
        out.append((t - PERIOD * d, t0, kind, i - d, n))
    return [(kind, m, n) for _, _, kind, m, n in sorted(out) if 0 <= m < B]


ITERATIONS = range(-3, B + 3)


def rounds(kinds, slots):
    order = []
    for i in ITERATIONS:
        for kind, m, n in iteration("tensor", i):
            key = (kind, m, n // 4 if kind == "DN" else n)
            if kind in kinds and (not order or order[-1] != key):
                order.append(key)
    assert len(order) == len(set(order))
    return {key: (k % slots, k, order[k - slots] if k >= slots else None) for k, key in enumerate(order)}


def walk(eng, name, step):
    tables = [rounds(RING, RING_SLOTS), rounds(MISC, 1)]

    def lookup(kind, m, n, t):
        if kind not in RING and kind not in MISC:
            return None
        table = tables[kind in MISC]
        n = n // 4 if kind == "DN" else n
        slot, no, before = table[kind, m, n]
        if t is not None:
            (_, no2, before2), last = table[kind, m + 2, n], LOOP_LAST - LOOP_FIRST - 1
            slot_z, no_z, before_z = table[kind, m + last, n]
            assert no_z == no + (no2 - no) * (last // 2) and slot_z == slot
            assert before_z == (before[0], before[1] + last, before[2])
            no = t * (no2 - no) + no
        if before is not None:
            before = (before[0], Img(t, before[1]), before[2])
        return slot, no, before

    def run(i, t=None):
        for kind, m, n in iteration(name, i):
            step(kind, Img(t, m), n, lookup(kind, m, n, t))

    for i in ITERATIONS:
        if i < LOOP_FIRST:
            run(i)
    with eng.Fori(0, (LOOP_LAST + 1 - LOOP_FIRST) // 2) as t:
        run(LOOP_FIRST, t)
        run(LOOP_FIRST + 1, t)
    for i in ITERATIONS:
        if i > LOOP_LAST:
            run(i)


def build(nc, x, gamma, beta, conv_taps, conv_rows, wq, wk, wv, wd, wd_b, we, eyec, eyem, mean4, pair, dsum, sel,
          p2c, tabdc, tabnc, tabkc, firstc, validc, out):
    ctx = ExitStack()
    with ctx:
        def sb(name, shape, dt=F32):
            return ctx.enter_context(nc.sbuf_tensor(name, shape, dt))

        def sem(name):
            return ctx.enter_context(nc.semaphore(name))

        eye_center = sb("eye_center", [128, 256])
        mean4_sb = sb("mean4_sb", [128, 128])
        eye_mean = sb("eye_mean", [128, 132])
        pair_sb = sb("pair_sb", [128, 66])
        dsum_sb = sb("dsum_sb", [128, 64])
        eye16 = sb("eye16", [128, 128], F16)
        sel16 = sb("sel16", [128, CH * G * 128], F16)
        p2 = sb("p2", [128, CH, 2, HPC, 33])
        tabd = sb("tabd", [128, 2, HW4])
        tabn = sb("tabn", [128, TILES, 2 * PT])
        tabk = sb("tabk", [PT, 2, SLOTS])
        first = sb("first", [PT, SLOTS * EXPERTS])
        conv_w = sb("conv_w", [128, 4, 128], BF16)
        wq16 = sb("wq16", [128, DH], F16)
        wk16 = sb("wk16", [128, DH], F16)
        we16 = sb("we16", [128, EXPERTS * C + EXPERTS], F16)
        small = sb("small", [128, 16])
        gamma_c, beta_c, dense_b = (small[:, k:k + 1] for k in range(3))
        conv_scale, conv_sum, conv_bias, conv_scale2 = (small[:, k:k + 1] for k in range(3, 7))
        minus_one, den_eps, bn_inv, bn_half = (small[:, k:k + 1] for k in range(7, 11))
        bn_gain = small[:, 11:12]
        bin_a = sb("bin_a", [128, B])
        bin_thr = sb("bin_thr", [128, B])
        power = sb("power", [128, B])
        xt = sb("xt", [PT, TILES * G * C])
        nat = sb("nat", [128, PITCH, PITCH], BF16)
        shifted = sb("shifted", [128, PITCH, PITCH], BF16)
        xres = sb("xres", [128, PATCHES])
        t1 = sb("t1", [128, 2, PATCHES])
        t1b = sb("t1b", [128, PATCHES])
        xc = [sb(f"xc{k}", [PT, SLOTS, C]) for k in (1, 2)]
        sq1 = sb("sq1", [PT, SLOTS, C])
        sq2 = sb("sq2", [PT, 2, 2 * G, C])
        xn = [sb(f"xn{k}", [PT, SLOTS, C]) for k in (1, 2)]
        parts = [sb(f"parts{k}", [PT, SLOTS, 2 * C], F16) for k in (1, 2)]
        ssum = [sb(f"ssum{k}", [PT, SLOTS]) for k in (1, 2)]
        varr = [sb(f"varr{k}", [PT, SLOTS]) for k in (1, 2)]
        rstd = [sb(f"rstd{k}", [PT, SLOTS]) for k in (1, 2)]
        xcs = sb("xcs", [PT, SLOTS, 2, C])
        z1 = sb("z1", [128, 2, SLOTS * PT], F16)
        z2 = sb("z2", [128, SLOTS * PT], F16)
        ebuf = sb("ebuf", [128, 2, 1024])
        kbuf = sb("kbuf", [PT, 2, 1024])
        ktsb = sb("ktsb", [128, DH])
        gmat = sb("gmat", [128, 2, CH, 2, C])
        dmat = sb("dmat", [128, 2, CH, 2, HEADS])
        qbuf = sb("qbuf", [128, CH, TILES, G * PT])
        dcs = sb("dcs", [128, HW4])
        den = sb("den", [128, HW4])
        r_high = sb("r_high", [128, HALFW], F16)
        rs = sb("rs", [128, 2, HW4], F16)
        pbuf = sb("pbuf", [128, 4, 2, PT])
        spread_r = sb("spread_r", [128, 2, HW4])
        mean2 = sb("mean2", [PT, SLOTS])
        t2 = sb("t2", [PT, 2, TILES * G * C])
        route = sb("route", [PT, 4, SLOTS * EXPERTS])
        rmax = sb("rmax", [PT, 6, SLOTS])
        gate = sb("gate", [PT, SLOTS * EXPERTS])
        prod = sb("prod", [PT, 2, 4, EXPERTS * C])
        ffn = sb("ffn", [PT, SLOTS, C])
        qflat = qbuf[:, :, :, :].rearrange("p a b c -> p (a b c)")
        stage = [qflat[0:PT, k * 3584:(k + 1) * 3584].rearrange("p (b f) -> p b f", b=4) for k in range(2)]
        at, views = 2 * 3584, {}
        for name, width in (("taps", 512), ("valid", 512), ("rows", 288), ("wqa", DH), ("wka", DH),
                            ("wea", 264), ("tmp", 512), ("sel", CH * 4 * 128)):
            views[name] = qflat[:, at:at + width]
            at += width
        assert at <= CH * TILES * G * PT
        wqb_s, wkb_s, web_s = ebuf[:, 0, 0:DH], ebuf[:, 0, DH:2 * DH], ebuf[:, 1, 0:264]
        wva_s, wvb_s = t1[0:32, 0, 0:DH], t1[0:32, 1, 0:DH]
        wd_s = t1b[0:32, 0:DH]
        wvr = xres[0:32, 0:128]
        views["rows2"] = xres[:, 256:256 + 9 * C]
        stats = dcs[:, 0:B * 12].rearrange("p (b k) -> p b k", b=B)
        mv = den[:, 0:B * 2].rearrange("p (b k) -> p b k", b=B)
        bw = den[:, 64:64 + 8 * B].rearrange("p (k b) -> p k b", k=8)

        ps = ctx.enter_context(nc.psum_tensor("ps", [128, 8, 512], F32))

        def ring(s):
            return ps[:, 2 * s:2 * s + 2, :]

        def misc():
            return ps[:, 2 * RING_SLOTS, :]

        kt_bank = ps[:, 2 * RING_SLOTS + 1, :]

        consts_in = sem("consts_in")
        eye_in = sem("eye_in")
        stage_in = [sem(f"stage_in{k}") for k in range(2)]
        stage_turned = sem("stage_turned")
        stage_read = sem("stage_read")
        pe_pre = sem("pe_pre")
        eye16_made = sem("eye16_made")
        dve_pre = sem("dve_pre")
        pool_pre = sem("pool_pre")
        act_pre = sem("act_pre")
        x_in = sem("x_in")
        shift_in = sem("shift_in")
        out_stored = sem("out_stored")
        ring_full = sem("ring_full")
        misc_full = sem("misc_full")
        dcs_made = sem("dcs_made")
        numer_made = sem("numer_made")
        binarized = sem("binarized")
        xres_made = sem("xres_made")
        t1_made = sem("t1_made")
        xc_made = [sem(f"xc_made{k}") for k in (1, 2)]
        piece_summed = sem("piece_summed")
        ssum_made = [sem(f"ssum_made{k}") for k in (1, 2)]
        var_made = [sem(f"var_made{k}") for k in (1, 2)]
        rstd_made = [sem(f"rstd_made{k}") for k in (1, 2)]
        xn_made = [sem(f"xn_made{k}") for k in (1, 2)]
        high_made = [sem(f"high_made{k}") for k in (1, 2)]
        parts_made = [sem(f"parts_made{k}") for k in (1, 2)]
        z_made = [sem(f"z_made{k}") for k in (1, 2)]
        xcs_made = sem("xcs_made")
        kexp_made = sem("kexp_made")
        qexp_made = sem("qexp_made")
        k_made = sem("k_made")
        q_made = sem("q_made")
        ktx_done = sem("ktx_done")
        kt_copied = sem("kt_copied")
        g_made = sem("g_made")
        den_made = sem("den_made")
        recip_made = sem("recip_made")
        rhigh_made = sem("rhigh_made")
        r_rows_made = sem("r_rows_made")
        r_made = sem("r_made")
        qr_made = sem("qr_made")
        r_copied = sem("r_copied")
        qp_made = sem("qp_made")
        t1b_made = sem("t1b_made")
        t2_made = sem("t2_made")
        centered = sem("centered")
        squared = sem("squared")
        route_step = sem("route_step")
        ratio_made = sem("ratio_made")
        gate_step = sem("gate_step")
        gate_made = sem("gate_made")
        prod_made = sem("prod_made")
        pool_add = sem("pool_add")
        ffn_made = sem("ffn_made")
        out_made = sem("out_made")

        def wait(eng, s, v):
            if not isinstance(v, int) or v > 0:
                eng.wait_ge(s, v)

        READ = {"K": (k_made, 14), "R": (qr_made, 7), "RP": (r_copied, 7), "Q": (q_made, 14), "G": (g_made, 2),
                "LG": (route_step, 16), "F": (prod_made, 7), "XC": (xc_made[0], 1), "ZT": (z_made[0], 2), "ZU": (z_made[1], 2),
                "XT": (xres_made, 2), "CV": (t1_made, 2), "DN": (dcs_made, 2), "SU": (den_made, 2),
                "NM": (numer_made, 7), "T2": (t2_made, 4)}

        block = ctx.enter_context(nc.Block())

        @block.sync
        def _(sp):
            sp.dma_start(eye_center[:, :], eyec).then_inc(eye_in, 16)
            for dst, src in ((mean4_sb[:, :], mean4), (views["rows"], conv_rows),
                             (small[:, 0:1], gamma), (small[:, 1:2], beta), (small[:, 2:3], wd_b)):
                sp.dma_start(dst, src).then_inc(consts_in, 16)
            x4 = x.rearrange("(q b) h w c -> q b (h w c)", b=4).rearrange("q b (p f) -> q p b f", p=PT)

            def stage_load(q, k, turned):
                wait(sp, stage_turned, turned)
                sp.dma_start(stage[k], q).then_inc(stage_in[k], 16)

            for k in range(2):
                stage_load(x4[k], k, 0)
            for dst, src in ((pair_sb[:, :], pair), (eye_mean[:, :], eyem), (dsum_sb[:, :], dsum), (views["taps"], conv_taps),
                             (views["valid"], validc), (views["wqa"], wq[0]), (wqb_s, wq[1]), (views["wka"], wk[0]),
                             (wkb_s, wk[1]), (views["wea"], we[0]), (web_s, we[1]), (wva_s, wv[0]), (wvb_s, wv[1]),
                             (wd_s, wd), (p2[:, :, :, :, :].rearrange("p a b c d -> p (a b c d)"), p2c),
                             (tabd[:, :, :].rearrange("p a b -> p (a b)"), tabdc), (tabk[:, :, :].rearrange("p a b -> p (a b)"), tabkc),
                             (first[:, :], firstc), (views["sel"], sel),
                             (tabn[:, :, :].rearrange("p a b -> p (a b)"), tabnc)):
                sp.dma_start(dst, src).then_inc(consts_in, 16)
            with sp.Fori(1, 4) as t:
                for k in range(2):
                    wait(sp, stage_turned, t * 8 + (4 * k - 4))
                    sp.dma_start(stage[k], x4[bass.ds(t * 2 + k, 1)].rearrange("q p b f -> (q p) b f"))\
                        .then_inc(stage_in[k], 16)

            xt_v = xt[:, :].rearrange("p (j d e) -> p j d e", j=TILES, d=2)

            def rows_of(a, m, yl):
                img = a[m.at(1):m.at(1) + 1] if m.t is None else a[bass.ds(m.at(1), 1)]
                return img.rearrange("b (q j d) (z e) c -> (b q) z (j d) (e c)", j=TILES, d=2, e=2)[yl]

            def load(m):
                for yl in range(YL):
                    sp.dma_start(xt_v[PR * yl:PR * yl + PR].rearrange("p j d e -> p (j d) e"), rows_of(x, m, yl))\
                        .then_inc(x_in, 16)

            def step(kind, m, n, rd):
                if kind == "XT" and n == 0:
                    wait(sp, xres_made, m.at(2))
                    load(m)
                if kind == "CV" and n == 0:
                    sp.wait_ge(binarized, m.at(2, 2))
                    for g in range(G):
                        dy, dx = g // 2, g % 2
                        q = slice(32 * g, 32 * g + 32)
                        src = nat[q, 1 - dy:1 - dy + PR + 1, 1 - dx:1 - dx + PR + 1]
                        sp.dma_start(shifted[q, 0:PR + 1, 0:PR + 1], src).then_inc(shift_in, 16)
                if kind == "OUT":
                    sp.wait_ge(out_made, m.at(1, 1))
                    for yl in range(YL):
                        src = ffn[PR * yl:PR * yl + PR, :, :].rearrange("p (a e) c -> p a (e c)", e=2)
                        sp.dma_start(rows_of(out, m, yl), src).then_inc(out_stored, 16)

            walk(sp, "sync", step)
            sp.wait_ge(out_stored, 16 * YL * B)

        @block.tensor
        def _(pe):
            eye = eye_center[:, 0:128]
            pe.wait_ge(eye_in, 16)
            def turn(t):
                for k in range(2):
                    pe.wait_ge(stage_in[k], t * 16 + 16)
                    for b in range(4):
                        wait(pe, stage_read, t * 8 + (4 * k + b - 3))
                        for j in range(TILES):
                            bank = 2 * b + (j >= 4)
                            dst = ps[:, bank, (j % 4) * PT:(j % 4 + 1) * PT]
                            mm = pe.transpose(dst, stage[k][:, b, j * 128:(j + 1) * 128], eye[0:PT, 0:PT])
                        mm.then_inc(stage_turned, 1)

            turn(0)
            with pe.Fori(1, 4) as t:
                turn(t)
            pe.wait_ge(consts_in, 16 * 25)
            pe.wait_ge(dve_pre, 1)
            pe.matmul(ps[:, 0, 0:B], mean4_sb[:, :], bw[:, 0, :], start=True, stop=True).then_inc(pe_pre, 1)
            pe.wait_ge(dve_pre, 2)
            pe.matmul(ps[:, 1, 0:B], mean4_sb[:, :], bw[:, 2, :], start=True, stop=True).then_inc(pe_pre, 1)
            for h in range(HEADS):
                pe.wait_ge(dve_pre, 3 + h)
                mm = pe.matmul(ps[:, 2, C * h:C * h + C], wvr[:, :] if h % 2 == 0 else xres[0:32, 128:256],
                               wd_s[:, C * h:C * h + C], start=True, stop=True)
                mm.then_inc(pe_pre, 1)

            def step(kind, m, n, rd):
                if rd:
                    slot, _, before = rd
                    o = ring(slot) if kind in RING else misc()
                    if before and not (kind == "DN" and n % 4):
                        k, image, r = before
                        pe.wait_ge(READ[k][0], image.at(READ[k][1], r + 1))
                if kind == "XT":
                    pe.wait_ge(x_in, m.at(64, 64))
                    for k in range(HALF[n]):
                        j = 4 * n + k
                        mm = pe.transpose(o[:, PT * k:PT * k + PT], xt[:, 128 * j:128 * j + 128], eye[0:PT, 0:PT])
                    mm.then_inc(misc_full, 1)
                elif kind == "CV":
                    pe.wait_ge(shift_in, m.at(64, 64))
                    w = HALF[n]
                    dst = o[:, 0:w * PT].rearrange("p (j y x) -> p j y x", j=w, y=YL)
                    for k in range(4):
                        di, dj = k // 2, k % 2
                        src = shifted[:, di:di + PR, dj:dj + PR].rearrange("p (y j) x -> p j y x", j=TILES)
                        mm = pe.matmul(dst, conv_w[:, k, :], src[:, 4 * n:4 * n + w], start=(k == 0), stop=(k == 3))
                    mm.then_inc(misc_full, 1)
                elif kind == "XC":
                    pe.wait_ge(t1_made, m.at(2, 2))
                    for j in range(TILES):
                        mm = pe.matmul(o[0:PT, j // 4, 128 * (j % 4):128 * (j % 4) + 128],
                                       t1[:, m.par, PT * j:PT * j + PT], eye_center[:, 128:256], start=True, stop=True)
                    mm.then_inc(ring_full, 1)
                elif kind in ("ZT", "ZU"):
                    ln = kind == "ZU"
                    pe.wait_ge(parts_made[ln], m.at(1, 1))
                    pe.wait_ge(eye16_made, 1)
                    of = o.bitcast(F16)
                    for k in range(14):
                        for q, w in (((0, 32), (32, 32), (64, 32), (96, 32)) if k == 0 else ((0, 64), (64, 64))):
                            mm = pe.matmul(of[q:q + w, k // 7, PT * (k % 7):PT * (k % 7) + PT],
                                           parts[ln][:, 14 * n + k, q % 64:q % 64 + w],
                                           eye16[0:PT, 0:PT], is_transpose=True, start=True, stop=True)
                    mm.then_inc(ring_full, 1)
                elif kind == "K":
                    pe.wait_ge(z_made[0], m.at(2, n // 7 + 1))
                    for k in range(2):
                        s = 2 * n + k
                        mm = pe.matmul(o[0:PT, k, :], z1[:, m.par, PT * s:PT * s + PT], wk16[:, :], start=True, stop=True)
                    mm.then_inc(ring_full, 1)
                elif kind == "KX":
                    pe.wait_ge(k_made, m.at(14, n + 1))
                    if n in (0, 7):
                        pe.wait_ge(xcs_made, m.at(2, n // 7 + 1))
                    if n == 0:
                        wait(pe, kt_copied, m.at(1))
                    for k in range(2):
                        mm = pe.matmul(kt_bank[64 * k:64 * k + 64, :],
                                       xcs[:, 2 * n + k, :, :].rearrange("p a c -> p (a c)"),
                                       kbuf[:, n % 2, DH * k:DH * k + DH], start=(n == 0), stop=(n == 13))
                    mm.then_inc(ktx_done, 1)
                elif kind == "G":
                    pe.wait_ge(kt_copied, m.at(1, 1))
                    for k in range(2):
                        for h in range(HPC):
                            a = HPC * (2 * n + k) + h
                            mm = pe.matmul(o[32 * h:32 * h + 32, k, 0:66].rearrange("p (a o) -> p a o", a=2),
                                           ktsb[:, 32 * a:32 * a + 32], p2[:, 2 * n + k, :, h, :],
                                           start=True, stop=True)
                    mm.then_inc(ring_full, 1)
                elif kind == "Q":
                    j, k0 = n // 2, 2 * (n % 2)
                    for k in range(2):
                        mm = pe.matmul(o[:, k, 0:G * PT], wq16[:, 128 * (k0 + k):128 * (k0 + k) + 128],
                                       z1[:, m.par, G * PT * j:G * PT * (j + 1)], start=True, stop=True)
                    mm.then_inc(ring_full, 1)
                elif kind == "DN":
                    h, c = n // 4, n % 4
                    pe.wait_ge(q_made, m.at(14, 8 * h + 8 if h == 0 else 14))
                    if n == 0:
                        pe.wait_ge(g_made, m.at(2, 2))
                    for j in range(HALF[h]):
                        mm = pe.matmul(o[32 * j:32 * j + 32, 0:HW4],
                                       dmat[:, m.par, c, :, :].rearrange("p a h -> p (a h)"),
                                       qbuf[:, c, 4 * h + j, :], start=(c == 0), stop=(c == CH - 1))
                    if c == CH - 1:
                        mm.then_inc(misc_full, 1)
                elif kind == "SU":
                    pe.wait_ge(dcs_made, m.at(2, n + 1))
                    for c in range(2):
                        mm = pe.matmul(o[64 * c:64 * c + 64, 0:HALFW], dsum_sb[:, :],
                                       dcs[:, HALFW * c:HALFW * (c + 1)], start=True, stop=True)
                    mm.then_inc(misc_full, 1)
                elif kind in ("R", "RP"):
                    j, k0 = n, 2 if kind == "RP" else 0
                    pe.wait_ge(r_made, m.at(2, 1 + j // 4))
                    pe.wait_ge(r_rows_made, m.at(2, 1 + j // 4))
                    for k in range(2):
                        a = 4 * (k0 + k) + j % 4
                        mm = pe.matmul(o[:, k, 0:HW4], sel16[:, 128 * a:128 * a + 128], rs[:, j // 4, :],
                                       start=True, stop=True)
                    mm.then_inc(ring_full, 1)
                elif kind == "NM":
                    pe.wait_ge(qr_made, m.at(7, n + 1))
                    pe.wait_ge(qp_made, m.at(7, n + 1))
                    for c in range(CH):
                        for v in range(2):
                            rhs = qbuf[:, c, n, :].rearrange("p (a v t) -> p a v t", a=2, v=2)[:, :, v, :]
                            mm = pe.matmul(o[64 * v:64 * v + 64, 0:2 * PT].rearrange("p (a t) -> p a t", a=2),
                                           gmat[:, m.par, c, :, :].rearrange("p a o -> p (a o)"), rhs,
                                           start=(c == 0), stop=(c == CH - 1))
                    mm.then_inc(misc_full, 1)
                elif kind == "T2":
                    tiles = range(2 * n, min(2 * n + 2, TILES))
                    pe.wait_ge(numer_made, m.at(7, tiles[-1] + 1))
                    if n == 0:
                        pe.wait_ge(t1b_made, m.at(1, 1))
                    for jj, j in enumerate(tiles):
                        dst = o[0:PT, 256 * jj:256 * jj + 132]
                        pe.matmul(dst, t1b[:, PT * j:PT * j + PT], eye_mean[:, :], start=True, stop=False)
                        for a in range(2):
                            mm = pe.matmul(dst[:, 66 * a:66 * a + 66], pbuf[:, j % 4, a, :], pair_sb[:, :],
                                           start=False, stop=(a == 1))
                    mm.then_inc(misc_full, 1)
                elif kind == "LG":
                    pe.wait_ge(z_made[1], m.at(2, 2))
                    for s in range(SLOTS):
                        mm = pe.matmul(o[0:PT, 0, EXPERTS * s:EXPERTS * s + EXPERTS], z2[:, PT * s:PT * s + PT],
                                       we16[:, EXPERTS * C:], start=True, stop=True)
                    mm.then_inc(ring_full, 1)
                elif kind == "F":
                    for k in range(4):
                        s = 4 * n + k
                        mm = pe.matmul(o[0:PT, k // 2, 256 * (k % 2):256 * (k % 2) + 256], z2[:, PT * s:PT * s + PT],
                                       we16[:, 0:EXPERTS * C], start=True, stop=True)
                    mm.then_inc(ring_full, 1)

            pe.wait_ge(dve_pre, 22)
            walk(pe, "tensor", step)

        @block.scalar
        def _(act):
            act.wait_ge(dve_pre, 19)
            for v in range(2):
                for cs in range(2):
                    q = slice(64 * v + 32 * cs, 64 * v + 32 * cs + 32)
                    dst = p2[q, :, cs, :, 0:C]
                    last = act.activation(dst, ps[q, 2, :].rearrange("p (a h o) -> p a h o", a=CH, h=HPC), ACT.Copy,
                                          scale=SHIFT)
            last.then_inc(act_pre, 1)
            act.wait_ge(dve_pre, 22)

            def step(kind, m, n, rd):
                if rd:
                    slot, no, _ = rd
                    o = ring(slot) if kind in RING else misc()
                if kind == "XT":
                    act.wait_ge(binarized, m.at(2, n + 1))
                    if n == 0:
                        wait(act, t1_made, m.at(2))
                    a, b = COL[n]
                    act.activation(xres[:, a:b], o[:, 0:b - a], ACT.Identity, bias=conv_bias).then_inc(xres_made, 1)
                elif kind == "XC":
                    act.wait_ge(ring_full, no + 1)
                    wait(act, xn_made[0], m.at(1))
                    wait(act, ssum_made[0], m.at(1))
                    for k in range(2):
                        a, w = 16 * k, 4 * HALF[k]
                        src = o[0:PT, k, 0:w * C].rearrange("p (s c) -> p s c", c=C)
                        act.activation(xc[0][:, a:a + w, :], src, ACT.Copy)
                        last = act.activation(sq1[:, a:a + w, :], src, ACT.Square)
                    last.then_inc(xc_made[0], 1)
                elif kind in ("XH1", "XH2"):
                    ln = kind == "XH2"
                    act.wait_ge(xn_made[ln], m.at(1, 1))
                    act.activation(parts[ln][:, :, 0:C], xn[ln][:, :, :], ACT.Copy).then_inc(high_made[ln], 1)
                elif kind in ("ZT", "ZU"):
                    ln = kind == "ZU"
                    act.wait_ge(ring_full, no + 1)
                    if ln and n == 0:
                        wait(act, prod_made, m.at(7))
                    dst = (z2 if ln else z1[:, m.par, :])[:, 14 * PT * n:14 * PT * (n + 1)]
                    act.activation(dst.rearrange("p (a b) -> p a b", a=2), o.bitcast(F16)[:, :, 0:7 * PT], ACT.Copy)\
                        .then_inc(z_made[ln], 1)
                elif kind == "K":
                    act.wait_ge(ring_full, no + 1)
                    wait(act, k_made, m.at(14, n))
                    act.activation(ebuf[0:PT, 0, :].rearrange("p (a b) -> p a b", a=2), o[0:PT, :, :], ACT.Exp,
                                   bias=minus_one[0:PT, :]).then_inc(kexp_made, 1)
                elif kind == "Q":
                    act.wait_ge(ring_full, no + 1)
                    wait(act, q_made, m.at(14, n))
                    act.activation(ebuf[:, 1, 0:2 * G * PT].rearrange("p (a b) -> p a b", a=2), o[:, :, 0:G * PT],
                                   ACT.Exp, bias=minus_one).then_inc(qexp_made, 1)
                elif kind == "KT":
                    act.wait_ge(ktx_done, m.at(14, 14))
                    act.activation(ktsb[:, :], kt_bank, ACT.Copy).then_inc(kt_copied, 1)
                elif kind == "G":
                    act.wait_ge(ring_full, no + 1)
                    src = o[:, :, 0:66].rearrange("p k (a o) -> p k a o", a=2)
                    act.activation(gmat[:, m.par, 2 * n:2 * n + 2, :, :], src[:, :, :, 0:C], ACT.Copy)
                    for h in range(HPC):
                        q = slice(32 * h, 32 * h + 32)
                        for k in range(2):
                            c = 2 * n + k
                            last = act.activation(dmat[q, m.par, c, :, HPC * c + h], src[q, k, :, C], ACT.Copy)
                    last.then_inc(g_made, 1)
                elif kind == "SU":
                    act.wait_ge(misc_full, no + 1)
                    wait(act, r_made, m.at(2, n))
                    act.activation(den[:, 0:HALFW], o[:, 0:HALFW], ACT.Identity, bias=den_eps).then_inc(den_made, 1)
                elif kind == "RC":
                    act.wait_ge(recip_made, m.at(2, n + 1))
                    wait(act, qr_made, m.at(7, -3 if n == 0 else 0))
                    act.activation(r_high[:, :], den[:, 0:HALFW], ACT.Copy).then_inc(rhigh_made, 1)
                    for c in range(2):
                        last = act.activation(rs[0:64, n, HALFW * c:HALFW * (c + 1)], den[64 * c:64 * c + 64, 0:HALFW],
                                              ACT.Copy)
                    last.then_inc(r_rows_made, 1)
                elif kind == "RP":
                    act.wait_ge(ring_full, no + 1)
                    wait(act, qp_made, m.at(7, n))
                    act.activation(spread_r[:, :, :], o[:, :, 0:HW4], ACT.Copy).then_inc(r_copied, 1)
                elif kind == "T2":
                    act.wait_ge(misc_full, no + 1)
                    if n == 0:
                        wait(act, out_made, m.at(1, -1))
                        wait(act, centered, m.at(4))
                    w = min(2, TILES - 2 * n)
                    src = o[0:PT, 0:256 * w].rearrange("p (j x) -> p j x", j=w)[:, :, 0:132]
                    src = src.rearrange("p j (a f) -> p j a f", a=2)
                    a = 2 * n
                    act.activation(t2[:, m.par, 128 * a:128 * (a + w)].rearrange("p (j a f) -> p j a f", j=w, a=2),
                                   src[:, :, :, 0:64], ACT.Copy)
                    act.activation(mean2[:, G * a:G * (a + w)].rearrange("p (j a v) -> p j a v", j=w, a=2),
                                   src[:, :, :, 64:66], ACT.Copy).then_inc(t2_made, 1)
                elif kind == "S2":
                    act.wait_ge(centered, m.at(4, n + 1))
                    wait(act, piece_summed, m.at(4, n - 1))
                    a, w = 2 * G * n, G * min(2, TILES - 2 * n)
                    act.activation(sq2[:, n % 2, 0:w, :], xc[1][:, a:a + w, :], ACT.Square).then_inc(squared, 1)
                elif kind == "TB":
                    act.wait_ge(t1_made, m.at(2, 2))
                    act.activation(t1b[:, :], t1[:, m.par, :], ACT.Identity, bias=dense_b).then_inc(t1b_made, 1)
                elif kind == "RT" and n == 5:
                    act.wait_ge(route_step, m.at(16, 13))
                    act.activation(rmax[:, 3, :], rmax[:, 2, :], ACT.Exp).then_inc(ratio_made, 1)

            walk(act, "scalar", step)

        @block.gpsimd
        def _(pool):
            nc.gpsimd.memset(power[:, :], -0.5).then_inc(pool_pre, 1)
            pool.wait_ge(pool_pre, 1)
            pool.wait_ge(dve_pre, 20)
            nc.gpsimd.tensor_tensor(bw[:, 4, :], bw[:, 3, :], power[:, :], ALU.pow).then_inc(pool_pre, 1)
            pool.wait_ge(dve_pre, 21)
            nc.gpsimd.tensor_tensor(bn_inv, bn_half, power[:, 0:1], ALU.pow).then_inc(pool_pre, 1)

            def step(kind, m, n, rd):
                if kind in ("PN1", "PN2"):
                    ln = kind == "PN2"
                    pool.wait_ge(var_made[ln], m.at(1, 1))
                    nc.gpsimd.tensor_tensor(rstd[ln][:, :], varr[ln][:, :], power[0:PT, 0:SLOTS], ALU.pow)\
                        .then_inc(rstd_made[ln], 1)
                    pool.wait_ge(rstd_made[ln], m.at(1, 1))
                    wait(pool, high_made[ln], m.at(1))
                    nc.gpsimd.tensor_tensor(xn[ln][:, :, 0:C - 1], xc[ln][:, :, 0:C - 1],
                                            rstd[ln][:, :].unsqueeze(2).to_broadcast([PT, SLOTS, C - 1]), ALU.mult)\
                        .then_inc(xn_made[ln], 1)
                elif kind in ("PL1", "PL2"):
                    ln = kind == "PL2"
                    pool.wait_ge(high_made[ln], m.at(1, 1))
                    nc.gpsimd.tensor_tensor(parts[ln][:, :, C:2 * C], xn[ln][:, :, :], parts[ln][:, :, 0:C],
                                            ALU.subtract).then_inc(parts_made[ln], 1)
                elif kind == "CS":
                    pool.wait_ge(xn_made[0], m.at(1, 1))
                    wait(pool, ktx_done, m.at(14, 7 * n - 7))
                    w = slice(14 * n, 14 * n + 14)
                    for k in range(2):
                        last = nc.gpsimd.tensor_tensor(xcs[:, w, k, :], xn[0][:, w, :],
                                                       tabk[:, k, w].unsqueeze(2).to_broadcast([PT, 14, C]), ALU.mult)
                    last.then_inc(xcs_made, 1)
                elif kind == "RP":
                    pool.wait_ge(r_copied, m.at(7, n + 1))
                    nc.gpsimd.tensor_tensor(qbuf[:, 2:4, n, :], spread_r[:, :, :], qbuf[:, 2:4, n, :], ALU.mult)\
                        .then_inc(qp_made, 1)
                elif kind == "T2":
                    pool.wait_ge(t2_made, m.at(4, n + 1))
                    a, w = 2 * G * n, G * min(2, TILES - 2 * n)
                    nc.gpsimd.tensor_tensor(xc[1][:, a:a + w, :],
                                            t2[:, m.par, C * a:C * (a + w)].rearrange("p (s c) -> p s c", c=C),
                                            mean2[:, a:a + w].unsqueeze(2).to_broadcast([PT, w, C]), ALU.subtract)\
                        .then_inc(centered, 1)
                elif kind == "GT":
                    shape = [PT, SLOTS, EXPERTS]
                    hot1, hot2 = (route[:, k, :].rearrange("p (s e) -> p s e", e=EXPERTS) for k in (1, 2))
                    pool.wait_ge(route_step, m.at(16, 16))
                    wait(pool, prod_made, m.at(7))
                    nc.gpsimd.tensor_tensor(hot1, hot1, rmax[:, 5, :].unsqueeze(2).to_broadcast(shape), ALU.mult)\
                        .then_inc(gate_step, 1)
                    nc.gpsimd.tensor_tensor(hot2, hot2, rmax[:, 4, :].unsqueeze(2).to_broadcast(shape), ALU.mult)\
                        .then_inc(gate_step, 1)
                    pool.wait_ge(gate_step, m.at(2, 2))
                    nc.gpsimd.tensor_tensor(gate[:, :], route[:, 1, :], route[:, 2, :], ALU.add).then_inc(gate_made, 1)
                elif kind == "OUT":
                    pool.wait_ge(ffn_made, m.at(7, 7))
                    f = ffn[:, :, :].rearrange("p s c -> p (s c)")
                    nc.gpsimd.tensor_tensor(f, f, t2[:, m.par, :], ALU.add).then_inc(out_made, 1)
                elif kind == "F":
                    pool.wait_ge(prod_made, m.at(7, n + 1))
                    if n == 0:
                        wait(pool, out_stored, m.at(64))
                    p = prod[:, n % 2, :, :]
                    nc.gpsimd.tensor_tensor(p[:, :, 0:4 * C], p[:, :, 0:4 * C], p[:, :, 4 * C:], ALU.add)\
                        .then_inc(pool_add, 1)
                    pool.wait_ge(pool_add, m.at(14, 2 * n + 1))
                    nc.gpsimd.tensor_tensor(p[:, :, 0:2 * C], p[:, :, 0:2 * C], p[:, :, 2 * C:4 * C], ALU.add)\
                        .then_inc(pool_add, 1)
                    pool.wait_ge(pool_add, m.at(14, 2 * n + 2))
                    nc.gpsimd.tensor_tensor(ffn[:, 4 * n:4 * n + 4, :], p[:, :, 0:C], p[:, :, C:2 * C], ALU.add)\
                        .then_inc(ffn_made, 1)

            walk(pool, "gpsimd", step)

        @block.vector
        def _(dve):
            own = [0]
            chain = sem("chain")

            def link(ins):
                own[0] += 1
                ins.then_inc(chain, 1)
                dve.wait_ge(chain, own[0])

            v = nc.vector
            v.memset(minus_one, -1.0)
            v.memset(den_eps, DEN_EPS * SHIFT)
            v.memset(nat[:, :, :], 1.0)
            v.memset(dmat[:, :, :, :, :], 0.0)
            for ln in range(2):
                link(v.memset(xn[ln][:, :, C - 1:C], 1.0))
            def measure(t):
                for k in range(2):
                    for b in range(4):
                        img = t * 8 + (4 * k + b)
                        dve.wait_ge(stage_turned, img + 1)
                        for h in range(2):
                            last = v.bn_stats(stats[:, bass.ds(img, 1), 6 * h:6 * h + 6].rearrange("p a k -> p (a k)"),
                                              ps[:, 2 * b + h, 0:HALF[h] * PT])
                        last.then_inc(stage_read, 1)

            with dve.Fori(0, 3) as t:
                measure(t)
            dve.wait_ge(consts_in, 16 * 25)
            rows, rows2, tmp = views["rows"], views["rows2"], views["tmp"]
            link(v.tensor_scalar(rows2, rows, -1.0, None, ALU.mult))
            link(v.tensor_tensor(rows2, rows2, rows, ALU.max))
            link(v.tensor_reduce(conv_scale, rows2, AX_X, ALU.add))
            link(v.tensor_scalar(conv_scale, conv_scale, 1.0 / (9 * C), None, ALU.mult))
            link(v.tensor_scalar(rows2, rows, 0.0, 2.0, ALU.is_ge, ALU.mult))
            link(v.tensor_scalar(rows2, rows2, -1.0, None, ALU.add))
            link(v.tensor_reduce(conv_sum, rows2, AX_X, ALU.add))
            link(v.tensor_tensor(conv_bias, conv_scale, conv_sum, ALU.mult))
            link(v.tensor_scalar(conv_bias, conv_bias, -1.0, None, ALU.mult))
            link(v.tensor_scalar(conv_scale2, conv_scale, 2.0, None, ALU.mult))
            link(v.tensor_scalar(tmp, views["taps"], 0.0, 2.0, ALU.is_ge, ALU.mult))
            link(v.tensor_scalar(tmp, tmp, -1.0, None, ALU.add))
            link(v.tensor_tensor(conv_w[:, :, :].rearrange("p a b -> p (a b)"), tmp, views["valid"], ALU.mult))
            for dst, a, b, w in ((wq16, views["wqa"], wqb_s, DH), (wk16, views["wka"], wkb_s, DH),
                                 (we16, views["wea"], web_s, 264)):
                link(v.tensor_tensor(a, a, b, ALU.subtract))
                link(v.tensor_copy(dst[:, 0:w], a))
                link(v.tensor_tensor(dst[64:128, 0:w], a[64:128], dst[64:128, 0:w], ALU.subtract))
            v.tensor_copy(eye16[:, :], eye_center[:, 0:128]).then_inc(eye16_made, 1)
            link(v.tensor_copy(sel16[:, :], views["sel"]))
            measure(3)
            dve.wait_ge(stage_read, B)
            for b in range(B):
                last = v.bn_aggr(mv[:, b, :], stats[:, b, :])
            link(last)
            v.tensor_copy(bw[:, 0, :], mv[:, :, 0]).then_inc(dve_pre, 1)
            dve.wait_ge(pe_pre, 1)
            link(v.tensor_copy(bw[:, 1, :], ps[:, 0, 0:B]))
            link(v.tensor_tensor(bw[:, 5, :], mv[:, :, 0], bw[:, 1, :], ALU.subtract))
            link(v.tensor_tensor(bw[:, 6, :], bw[:, 5, :], bw[:, 5, :], ALU.mult))
            v.tensor_tensor(bw[:, 2, :], mv[:, :, 1], bw[:, 6, :], ALU.add).then_inc(dve_pre, 1)
            link(v.tensor_tensor(wva_s, wva_s, wvb_s, ALU.subtract))
            for h in range(HEADS):
                if h >= 2:
                    dve.wait_ge(pe_pre, 2 + h - 1)
                o = 128 * (h % 2)
                v.tensor_copy(xres[0:32, o:o + 128].rearrange("p (k a) -> p k a", k=4),
                              wva_s[:, C * h:C * h + C].unsqueeze(1).to_broadcast([32, 4, C])).then_inc(dve_pre, 1)
            dve.wait_ge(pe_pre, 2 + HEADS)
            v.tensor_scalar(minus_one, minus_one, 1.0, None, ALU.mult).then_inc(dve_pre, 1)
            link(v.tensor_scalar(bw[:, 3, :], ps[:, 1, 0:B], GN_EPS, None, ALU.add))
            link(v.tensor_copy(bw[:, 7, :], ps[:, 1, 0:B]))
            v.tensor_copy(small[:, 12:13], small[:, 0:1]).then_inc(dve_pre, 1)
            dve.wait_ge(pool_pre, 2)
            link(v.tensor_tensor(bw[:, 5, :], bw[:, 7, :], bw[:, 4, :], ALU.mult))
            link(v.tensor_tensor(bw[:, 6, :], bw[:, 5, :], bw[:, 4, :], ALU.mult))
            link(v.tensor_reduce(bn_gain, bw[:, 6, :], AX_X, ALU.add))
            v.tensor_scalar(bn_half, bn_gain, 1.0 / B, BN_EPS, ALU.mult, ALU.add).then_inc(dve_pre, 1)
            dve.wait_ge(pool_pre, 3)
            link(v.tensor_tensor(bn_gain, bn_inv, gamma_c, ALU.mult))
            link(v.tensor_scalar(bin_a[:, :], bw[:, 4, :], bn_gain, None, ALU.mult))
            link(v.tensor_tensor(bw[:, 5, :], bin_a[:, :], bw[:, 1, :], ALU.mult))
            link(v.tensor_scalar(bin_thr[:, :], bw[:, 5, :], beta_c, None, ALU.subtract))
            dve.wait_ge(act_pre, 1)
            v.tensor_copy(small[:, 12:13], small[:, 0:1]).then_inc(dve_pre, 1)

            def step(kind, m, n, rd):
                if rd:
                    slot, no, _ = rd
                    o = ring(slot) if kind in RING else misc()
                if kind == "XT":
                    dve.wait_ge(misc_full, no + 1)
                    if n == 0:
                        wait(dve, shift_in, m.at(64))
                    w = HALF[n]
                    dst = nat[:, 1:1 + PR, 1:1 + PR].rearrange("p (y j) x -> p j y x", j=TILES)[:, 4 * n:4 * n + w]
                    i = bass.ds(m.at(1), 1) if m.t is not None else slice(m.c, m.c + 1)
                    for y in range(YL):
                        last = v.tensor_scalar(dst[:, :, y, :],
                                               o[:, 0:w * PT].rearrange("p (j y x) -> p j y x", j=w, y=YL)[:, :, y, :],
                                               bin_a[:, i], bin_thr[:, i], ALU.mult, ALU.is_ge)
                    last.then_inc(binarized, 1)
                elif kind == "CV":
                    dve.wait_ge(misc_full, no + 1)
                    dve.wait_ge(xres_made, m.at(2, n + 1))
                    if n == 0:
                        wait(dve, t1b_made, m.at(1, -1))
                    a, b = COL[n]
                    v.scalar_tensor_tensor(t1[:, m.par, a:b], o[:, 0:b - a], conv_scale2, xres[:, a:b], ALU.mult,
                                           ALU.add).then_inc(t1_made, 1)
                elif kind in ("SM1", "SM2"):
                    ln = kind == "SM2"
                    if ln:
                        dve.wait_ge(piece_summed, m.at(4, 4))
                    else:
                        dve.wait_ge(xc_made[0], m.at(1, 1))
                        v.tensor_reduce(ssum[0][:, :], sq1[:, :, :], AX_X, ALU.add).then_inc(ssum_made[0], 1)
                        dve.wait_ge(ssum_made[0], m.at(1, 1))
                    wait(dve, rstd_made[ln], m.at(1))
                    v.tensor_scalar(varr[ln][:, :], ssum[ln][:, :], 1.0 / C, LN_EPS, ALU.mult, ALU.add)\
                        .then_inc(var_made[ln], 1)
                elif kind == "S2":
                    dve.wait_ge(squared, m.at(4, n + 1))
                    w = G * min(2, TILES - 2 * n)
                    v.tensor_reduce(ssum[1][:, 2 * G * n:2 * G * n + w], sq2[:, n % 2, 0:w, :], AX_X, ALU.add)\
                        .then_inc(piece_summed, 1)
                elif kind == "K":
                    dve.wait_ge(kexp_made, m.at(14, n + 1))
                    wait(dve, ktx_done, m.at(14, n - 1))
                    v.scalar_tensor_tensor(kbuf[:, n % 2, :].rearrange("p (a b) -> p a b", a=2), o[0:PT, :, :], 1.0,
                                           ebuf[0:PT, 0, :].rearrange("p (a b) -> p a b", a=2), ALU.max, ALU.min)\
                        .then_inc(k_made, 1)
                elif kind == "Q":
                    j, k0 = n // 2, 2 * (n % 2)
                    dve.wait_ge(qexp_made, m.at(14, n + 1))
                    v.scalar_tensor_tensor(qbuf[:, k0:k0 + 2, j, :], o[:, :, 0:G * PT], 1.0,
                                           ebuf[:, 1, 0:2 * G * PT].rearrange("p (a b) -> p a b", a=2), ALU.max,
                                           ALU.min).then_inc(q_made, 1)
                elif kind == "DN" and n % 4 == 3:
                    h = n // 4
                    dve.wait_ge(misc_full, no + 1)
                    wait(dve, den_made, m.at(2, h))
                    q = slice(0, 32 * HALF[h])
                    v.tensor_tensor(dcs[q, :], o[q, 0:HW4], tabd[q, h, :], ALU.mult).then_inc(dcs_made, 1)
                elif kind == "RC":
                    dve.wait_ge(den_made, m.at(2, n + 1))
                    v.reciprocal(den[:, 0:HALFW], den[:, 0:HALFW]).then_inc(recip_made, 1)
                elif kind == "RL":
                    dve.wait_ge(rhigh_made, m.at(2, n + 1))
                    for c in range(2):
                        q = slice(64 * c, 64 * c + 64)
                        last = v.tensor_tensor(rs[64:128, n, HALFW * c:HALFW * (c + 1)], den[q, 0:HALFW], r_high[q, :],
                                               ALU.subtract)
                    last.then_inc(r_made, 1)
                elif kind == "R":
                    dve.wait_ge(ring_full, no + 1)
                    v.tensor_tensor(qbuf[:, 0:2, n, :], o[:, :, 0:HW4], qbuf[:, 0:2, n, :], ALU.mult)\
                        .then_inc(qr_made, 1)
                elif kind == "NM":
                    dve.wait_ge(misc_full, no + 1)
                    wait(dve, t2_made, m.at(4, (n - 4) // 2 + 1 if n >= 4 else 0))
                    v.tensor_tensor(pbuf[:, n % 4, :, :].rearrange("p a t -> p (a t)"), o[:, 0:2 * PT],
                                    tabn[:, n, :], ALU.mult).then_inc(numer_made, 1)
                elif kind == "LG":
                    dve.wait_ge(ring_full, no + 1)
                    v.tensor_copy(route[:, 0, :], o[0:PT, 0, 0:SLOTS * EXPERTS]).then_inc(route_step, 1)
                elif kind == "RT":
                    shape = [PT, SLOTS, EXPERTS]

                    def grid(a):
                        return a.rearrange("p (s e) -> p s e", e=EXPERTS)

                    def spread(a):
                        return a.unsqueeze(2).to_broadcast(shape)

                    logits, hot1, hot2, rest = (route[:, k, :] for k in range(4))
                    top1, top2, diff, ratio, w1, w2 = (rmax[:, k, :] for k in range(6))

                    def after(k):
                        dve.wait_ge(route_step, m.at(16, k))

                    if n == 0:
                        wait(dve, gate_made, m.at(1))
                    if n in (0, 3):
                        top, src, hot, w, k = (top1, logits, hot1, w1, 1) if n == 0 else (top2, rest, hot2, w2, 7)
                        after(k)
                        v.tensor_reduce(top, grid(src), AX_X, ALU.max).then_inc(route_step, 1)
                        after(k + 1)
                        v.tensor_tensor(grid(hot), grid(src), spread(top), ALU.is_equal).then_inc(route_step, 1)
                    elif n in (1, 4):
                        hot, w, k = (hot1, w1, 3) if n == 1 else (hot2, w2, 9)
                        after(k)
                        v.tensor_tensor(hot, hot, first[:, :], ALU.mult).then_inc(route_step, 1)
                        after(k + 1)
                        v.tensor_reduce(w, grid(hot), AX_X, ALU.max).then_inc(route_step, 1)
                    elif n == 2:
                        after(5)
                        v.tensor_tensor(grid(hot1), grid(hot1), spread(w1), ALU.is_equal).then_inc(route_step, 1)
                        after(6)
                        v.scalar_tensor_tensor(rest, hot1, -3.0e38, logits, ALU.mult, ALU.add).then_inc(route_step, 1)
                    elif n == 5:
                        after(11)
                        v.tensor_tensor(grid(hot2), grid(hot2), spread(w2), ALU.is_equal).then_inc(route_step, 1)
                        v.tensor_tensor(diff, top2, top1, ALU.subtract).then_inc(route_step, 1)
                    elif n == 6:
                        dve.wait_ge(ratio_made, m.at(1, 1))
                        v.tensor_scalar(w1, ratio, 1.0, None, ALU.add).then_inc(route_step, 1)
                        after(14)
                        v.reciprocal(w2, w1).then_inc(route_step, 1)
                        after(15)
                        v.tensor_tensor(w1, ratio, w2, ALU.mult).then_inc(route_step, 1)
                elif kind == "F":
                    dve.wait_ge(ring_full, no + 1)
                    if n == 0:
                        dve.wait_ge(gate_made, m.at(1, 1))
                    wait(dve, ffn_made, m.at(7, max(n - 1, 0)))
                    w = 4 * EXPERTS
                    v.tensor_tensor(prod[:, n % 2, :, :].rearrange("p s (e c) -> p (s e) c", c=C),
                                    o[0:PT, :, :].rearrange("p k (s c) -> p (k s) c", c=C),
                                    gate[:, w * n:w * n + w].unsqueeze(2).to_broadcast([PT, w, C]), ALU.mult)\
                        .then_inc(prod_made, 1)
            walk(dve, "vector", step)


def kernel(**inputs):
    import numpy as _np
    import concourse.bacc as _bacc
    from concourse import mybir as _mybir
    from concourse.bass_utils import run_bass_kernel_spmd as _run

    get = {k: _np.ascontiguousarray(v) for k, v in inputs.items()}
    f = _np.float32

    def column(a):
        return _np.ascontiguousarray(_np.tile(a, G)[:, None])

    def folded(w, b, const, copies):
        n = w.shape[1]
        a = _np.concatenate([w[0:C - 1], b[None, :]], 0)
        r = _np.concatenate([_np.tile(w[C - 1:C], (C - 1, 1)), _np.full((1, n), const, f)], 0)
        return _np.stack([_np.tile(a, (copies, 1)), _np.tile(r, (copies, 1))])

    conv = get["L0_conv_W"]
    taps = _np.zeros((G, C, 2, 2, G, C), f)
    for kh, kw, gi, i, j, go in _taps():
        taps[gi, :, i, j, go, :] = conv[kh, kw]
    rows = _np.tile(conv.reshape(9 * C, C).T, (G, 1))
    wq = folded(get["L1_attn_wq_w"].T, get["L1_attn_wq_b"], -1.0, 4)
    wk = folded(get["L1_attn_wk_w"].T, get["L1_attn_wk_b"], -1.0, 4)
    wv = folded(get["L1_attn_wv_w"].T, get["L1_attn_wv_b"], 0.0, 1)
    wv = wv.reshape(2, C, HEADS, C).transpose(0, 3, 2, 1).reshape(2, C, DH)
    wd = get["L1_attn_dense_w"].reshape(C, HEADS, C).transpose(2, 1, 0).reshape(C, DH)
    expert = get["L1_ffn_expert_w"].transpose(1, 0, 2).reshape(C, EXPERTS * C)
    we = folded(_np.concatenate([expert, get["L1_ffn_router_w"]], 1),
                _np.concatenate([get["L1_ffn_expert_b"].reshape(-1), get["L1_ffn_router_b"]]), 0.0, 4)
    c = consts()
    arrays = dict(x=get["x"], gamma=column(get["L0_conv_gamma"]), beta=column(get["L0_conv_beta"]),
                  conv_taps=taps.reshape(128, 512), conv_rows=rows, wq=wq, wk=wk, wv=wv, wd=wd,
                  wd_b=column(get["L1_attn_dense_b"]), we=we, eyec=c["eyec"], eyem=c["eyem"], mean4=c["mean4"], pair=c["pair"],
                  dsum=c["dsum"], sel=c["sel"], p2c=c["p2"], tabdc=c["tabd"], tabnc=c["tabn"], tabkc=c["tabk"],
                  firstc=c["first"], validc=c["valid"])
    nc = _bacc.Bacc("TRN2", target_bir_lowering=False, num_devices=1)
    arrays = {k: _np.ascontiguousarray(a) for k, a in arrays.items()}
    args = {k: nc.dram_tensor(f"in_{k}", a.shape, _mybir.dt.from_np(a.dtype), kind="ExternalInput").ap()
            for k, a in arrays.items()}
    out = nc.dram_tensor("out_0", (B, HW, HW, C), F32, kind="ExternalOutput").ap()
    build(nc, out=out, **args)
    r = _run(nc, [{f"in_{k}": a for k, a in arrays.items()}], core_ids=[0])
    return r.results[0]["out_0"]
```
